# Optimizing a Trainium2 kernel written in Bass

```python
import numpy as np
import jax
import jax.numpy as jnp

def _softmax(x, axis=-1):
    return jax.nn.softmax(x, axis=axis)

def _gelu(x):
    return jax.nn.gelu(x, approximate=True)

def _silu(x):
    return jax.nn.silu(x)

def _sigmoid(x):
    return jax.nn.sigmoid(x)

def _layernorm(x, axis=-1, eps=1e-05):
    m = jnp.mean(x, axis=axis, keepdims=True)
    v = jnp.var(x, axis=axis, keepdims=True)
    return (x - m) / jnp.sqrt(v + eps)

def _scatter_add(tgt, idx, src, axis=0):
    return tgt.at[idx].add(src)

def _segment_sum(src, seg, n):
    return jax.ops.segment_sum(src, seg, n)
kernel_name = 'mk_recurrent_d1_jaxref_r4_da2846'

def setup_inputs(seed: int=0):
    np.random.seed(seed)
    _w = jnp.asarray

    def _L0_attn_setup():
        import jax, jax.numpy as jnp
        import numpy as np
        D_IN = 512
        D_OUT = 512
        NUM_HEADS = 16
        HEAD_DIM = D_OUT // NUM_HEADS
        BLOCK_SIZE = 512
        BATCH = 4
        key = jax.random.key(seed)
        k_x, k_q, k_k, k_v, k_o = jax.random.split(key, 5)
        scale = 1.0 / np.sqrt(D_IN)
        return {'x': jax.random.normal(k_x, (BATCH, BLOCK_SIZE, D_IN), dtype=jnp.float32), 'Wq': jax.random.normal(k_q, (D_OUT, D_IN), dtype=jnp.float32) * scale, 'Wk': jax.random.normal(k_k, (D_OUT, D_IN), dtype=jnp.float32) * scale, 'Wv': jax.random.normal(k_v, (D_OUT, D_IN), dtype=jnp.float32) * scale, 'Wo': jax.random.normal(k_o, (D_OUT, D_OUT), dtype=jnp.float32) * scale}
    _L0_attn_in = _L0_attn_setup()

    def _L0_ffn_setup():
        import jax, jax.numpy as jnp
        import numpy as np
        B, S, D, H = (4, 512, 512, 2048)

        def fwht(x):
            orig_shape = x.shape
            n = orig_shape[-1]
            x = x.reshape(-1, n)
            h = 1
            while h < n:
                xb = x.reshape(-1, n // (2 * h), 2, h)
                a = xb[:, :, 0, :]
                b = xb[:, :, 1, :]
                x = jnp.stack([a + b, a - b], axis=2).reshape(-1, n)
                h *= 2
            scale = jnp.asarray(1.0 / np.sqrt(n), dtype=x.dtype)
            return (x * scale).reshape(orig_shape)
        key = jax.random.key(seed)
        kx, k1, k2, k3 = jax.random.split(key, 4)
        x = jax.random.normal(kx, (B, S, D), dtype=jnp.float32)
        W1 = jax.random.normal(k1, (H, D), dtype=jnp.float32) * (1.0 / np.sqrt(D))
        W2 = jax.random.normal(k2, (D, H), dtype=jnp.float32) * (1.0 / np.sqrt(H))
        W3 = jax.random.normal(k3, (H, D), dtype=jnp.float32) * (1.0 / np.sqrt(D))
        return {'x': x, 'W1': W1, 'W2': W2, 'W3': W3}
    _L0_ffn_in = _L0_ffn_setup()
    _d = {'L0_attn_x': _L0_attn_in['x'], 'L0_attn_Wq': _L0_attn_in['Wq'], 'L0_attn_Wk': _L0_attn_in['Wk'], 'L0_attn_Wv': _L0_attn_in['Wv'], 'L0_attn_Wo': _L0_attn_in['Wo'], 'L0_ffn_W1': _L0_ffn_in['W1'], 'L0_ffn_W2': _L0_ffn_in['W2'], 'L0_ffn_W3': _L0_ffn_in['W3']}
    _x0 = _d['L0_attn_x']
    _d['L0_attn_x'] = jax.random.normal(jax.random.fold_in(jax.random.key(seed), 1), (2, 1024, 512), dtype=_x0.dtype)
    del _x0
    return _d

def reference(L0_attn_x, L0_attn_Wq, L0_attn_Wk, L0_attn_Wv, L0_attn_Wo, L0_ffn_W1, L0_ffn_W2, L0_ffn_W3):

    def _L0_attn_ref(x, Wq, Wk, Wv, Wo):
        import jax, jax.numpy as jnp
        import numpy as np
        D_IN = 512
        D_OUT = 512
        NUM_HEADS = 16
        HEAD_DIM = D_OUT // NUM_HEADS
        BLOCK_SIZE = 512
        BATCH = 4
        b, t, _ = x.shape

        def proj(W):
            return (x @ W.T).reshape(b, t, NUM_HEADS, HEAD_DIM).transpose(0, 2, 1, 3)
        q, k, v = (proj(Wq), proj(Wk), proj(Wv))
        scores = jnp.einsum('bhqd,bhkd->bhqk', q, k) / jnp.sqrt(jnp.float32(HEAD_DIM))
        causal = jnp.triu(jnp.ones((t, t), dtype=bool), k=1)
        scores = jnp.where(causal, -jnp.inf, scores)
        attn = jax.nn.softmax(scores, axis=-1)
        ctx = jnp.einsum('bhqk,bhkd->bhqd', attn, v)
        ctx = ctx.transpose(0, 2, 1, 3).reshape(b, t, D_OUT)
        return ctx @ Wo.T

    def _L0_ffn_ref(x, W1, W2, W3):
        import jax, jax.numpy as jnp
        import numpy as np
        B, S, D, H = (4, 512, 512, 2048)

        def fwht(x):
            orig_shape = x.shape
            n = orig_shape[-1]
            x = x.reshape(-1, n)
            h = 1
            while h < n:
                xb = x.reshape(-1, n // (2 * h), 2, h)
                a = xb[:, :, 0, :]
                b = xb[:, :, 1, :]
                x = jnp.stack([a + b, a - b], axis=2).reshape(-1, n)
                h *= 2
            scale = jnp.asarray(1.0 / np.sqrt(n), dtype=x.dtype)
            return (x * scale).reshape(orig_shape)
        up_gate = jnp.einsum('bsd,hd->bsh', x, W1)
        up_lin = jnp.einsum('bsd,hd->bsh', x, W3)
        hidden = jax.nn.silu(up_gate) * up_lin
        hidden = fwht(hidden)
        out = jnp.einsum('bsh,dh->bsd', hidden, W2)
        return out
    x = L0_attn_x
    xn = _layernorm(x, axis=-1)
    s = _L0_attn_ref(xn, L0_attn_Wq, L0_attn_Wk, L0_attn_Wv, L0_attn_Wo)
    g = _silu(_L0_ffn_ref(xn, L0_ffn_W1, L0_ffn_W2, L0_ffn_W3))
    x = x + s * g
    return x

_drawn_inputs = setup_inputs


def setup_inputs(seed=0):
    import zlib

    import numpy as np

    out = dict(_drawn_inputs(seed))
    spreads = {}
    factors = {}
    for name, (base, spread) in spreads.items():
        noise = np.random.default_rng([zlib.crc32(name.encode()), seed]).standard_normal(out[name].shape)
        drawn = base * np.exp(spread * noise) if base else spread * noise
        out[name] = jnp.asarray(drawn.astype(out[name].dtype))
    for name, factor in factors.items():
        out[name] = (out[name] * factor).astype(out[name].dtype)
    return out
```

```python
import concourse.bass as bass
from concourse import mybir
from contextlib import ExitStack

F32 = mybir.dt.float32
F32R = mybir.dt.float32r
F16 = mybir.dt.float16
BF16 = mybir.dt.bfloat16
ALU = mybir.AluOpType
ACT = mybir.ActivationFunctionType
AX = mybir.AxisListType

P = 128
B, S, D = 2, 1024, 512
HID = 2048
NH, DH = 16, 32
KT = D // P
JT = HID // P
NT = S // P
W = 512
NC = S // W
TPC = W // P
SCALE = float(DH) ** -0.5
EPS = 1e-5
W2_SCALE = 0.5 * float(HID) ** -0.5
MASKED = -1e38
VC = 98
VS = 3 * DH
STACK = 3 * DH
STEPS = [(c, k) for c in range(NC) for k in range(TPC * (c + 1))]
NS = len(STEPS)
MAX_ORDER = [7, 0, 6, 1, 5, 2, 4, 3]
MAX_SLOT = 3
GROUPS = 4
GMM = 3 * KT
FFN_UPTO = [6, 9, 12, 15, 18, 21, 24, 27, 30, 33, 36, 38, 42, 48]
TANH_AT = {5: 0, 12: 1}


def build(nc, x, wq, wk, wv, wo, w1, w3, w2, hadamard, out):
    qk_dram = nc.dram_tensor("qk_parts", [2, 2, D, S], F32R, kind="Internal").ap()
    w2b_dram = nc.dram_tensor("w2_butterflied", [JT, P, D], F32, kind="Internal").ap()
    g_dram = nc.dram_tensor("w2_transformed", [2, P, JT, D], F32R, kind="Internal").ap()

    ctx = ExitStack()
    with ctx:
        def sb(name, shape, dt, stack=ctx):
            return stack.enter_context(nc.sbuf_tensor(name, shape, dt))

        def bank(name, banks=1):
            return ctx.enter_context(nc.psum_tensor(name, [P, banks, W], F32))

        def sem(name):
            return ctx.enter_context(nc.semaphore(name))

        ident = sb("ident", [P, P], F32)
        had = sb("had", [P, P], F32)
        causal = sb("causal", [P, S], BF16)
        ctx_nat = sb("ctx_nat", [P, NT, D], F32)
        stage = [sb(f"stage{i}", [P, D], F32) for i in range(3)]
        stats = sb("stats", [P, NT, 6], F32)
        mv = sb("mv", [P, NT, 2], F32)
        var, std, rstd, tmp = (sb(n, [P, NT], F32) for n in ("var", "std", "rstd", "tmp"))

        with ExitStack() as r:
            hidden = sb("hidden", [P, JT, S], F32, r)
        w_hi = [sb(f"w{m}_hi", [P, KT, D], F32R) for m in range(3)]
        w_lo = [sb(f"w{m}_lo", [P, KT, D], F32R) for m in range(3)]
        xb = sb("xb", [P, NT, D], F32)

        with ExitStack() as r:
            xt_hi = sb("xt_hi", [P, KT, S], F32R, r)
            xt_lo = sb("xt_lo", [P, KT, S], F32R, r)
            vparts = sb("vparts", [P, NT, NH, VC], BF16, r)
            with ExitStack() as q:
                wht_in = [sb(f"wht_in{i}", [P, JT, P], F32, q) for i in range(2)]
                wht_mid = sb("wht_mid", [P, JT, P], F32, q)
                qk_hi = [sb(f"qk_hi{i}", [P, W], F32R, q) for i in range(2)]
                qk_lo = [sb(f"qk_lo{i}", [P, W], F32R, q) for i in range(2)]
                vrest = [sb(f"vrest{i}", [P, W], F32, q) for i in range(2)]
            q_st = [sb(f"q_st{i}", [P, S], F32R, r) for i in range(2)]
            k_st = [sb(f"k_st{i}", [P, S], F32R, r) for i in range(2)]
            w13 = sb("w13", [P, 2, D], F32, r)
            w13_hi = [sb(f"w13_hi{i}", [P, 2, D], F32R, r) for i in range(2)]
            w13_lo = [sb(f"w13_lo{i}", [P, 2, D], F32R, r) for i in range(2)]
            expd = [sb(f"expd{i}", [P, W], F32, r) for i in range(3)]
            p_hi = [sb(f"p_hi{i}", [P, W], F16, r) for i in range(3)]
            p_lo = [sb(f"p_lo{i}", [P, W], F16, r) for i in range(3)]
            gate_t = sb("gate_t", [P, W], F32, r)
            gate_a = sb("gate_a", [P, W], F32, r)
            unused = [sb(f"unused{i}", [P, S], BF16, r) for i in range(2)]
            vh = [sb(f"vh{i}", [P, NT, VC], BF16, r) for i in range(2)]
            mx = sb("mx", [P, NT], F32, r)
            m_hi = sb("m_hi", [NT, P], F32R, r)
            m_lo = sb("m_lo", [NT, P], F32R, r)
            ctx_raw = [sb(f"ctx_raw{i}", [P, TPC, DH], F32, r) for i in range(NC)]
            rden = [sb(f"rden{i}", [P, TPC], F32, r) for i in range(NC)]
        g_hi = sb("g_hi", [P, JT, D], F32R)
        g_lo = sb("g_lo", [P, JT, D], F32R)
        h_hi = [sb(f"h_hi{i}", [P, JT // 2, P], F32R) for i in range(2)]
        h_lo = [sb(f"h_lo{i}", [P, JT // 2, P], F32R) for i in range(2)]
        wo_hi = sb("wo_hi", [P, KT, D], F32R)
        wo_lo = sb("wo_lo", [P, KT, D], F32R)
        ct_hi = [sb(f"ct_hi{i}", [P, KT, P], F32R) for i in range(2)]
        ct_lo = [sb(f"ct_lo{i}", [P, KT, P], F32R) for i in range(2)]
        x_in = [sb(f"x_in{i}", [P, D], F32) for i in range(2)]
        y = [sb(f"y{i}", [P, D], F32) for i in range(2)]

        F = [bank("f0"), bank("f1")]
        SB = [bank("s0"), bank("s1")]
        M = bank("m", 2)
        X = bank("xs")
        O = bank("o")

        const_ready = sem("const_ready")
        had_in = sem("had_in")
        phase_done = sem("phase_done")
        x_loaded = [sem(f"x_loaded{i}") for i in range(NT // 2)]
        stage_in = [sem(f"stage_in{i}") for i in range(3)]
        split_hi, split_lo = sem("split_hi"), sem("split_lo")
        stats_done, mv_done, var_done, sqrt_done, newton = (
            sem(n) for n in ("stats_done", "mv_done", "var_done", "sqrt_done", "newton"))
        xn_done, xt_ps, xt_hi_done, xt_lo_done = (
            sem(n) for n in ("xn_done", "xt_ps", "xt_hi_done", "xt_lo_done"))
        proj_ps, proj_hi_done, proj_lo_done = (sem(n) for n in ("proj_ps", "proj_hi_done", "proj_lo_done"))
        v2_done, v3_done = sem("v2_done"), sem("v3_done")
        qk_stored = [sem(f"qk_stored{i}") for i in range(2)]
        wht_loaded, wht_step, wht_stored = sem("wht_loaded"), sem("wht_step"), sem("wht_stored")
        ones_ready = sem("ones_ready")
        stack_in = [sem(f"stack_in{i}") for i in range(2)]
        max_ps, max_done, mt_ps, m_hi_done, m_lo_done, m_in = (
            sem(n) for n in ("max_ps", "max_done", "mt_ps", "m_hi_done", "m_lo_done", "m_in"))
        scores_ps, exp_done, mask_done, p_hi_done, p_lo_done, pv_done = (
            sem(n) for n in ("scores_ps", "exp_done", "mask_done", "p_hi_done", "p_lo_done", "pv_done"))
        max_begun, mask_begun = sem("max_begun"), sem("mask_begun")
        o_read, ctx_done, vh_ready = sem("o_read"), sem("ctx_done"), sem("vh_ready")
        w13_in, w13_hi_done, w13_lo_done = sem("w13_in"), sem("w13_hi_done"), sem("w13_lo_done")
        ffn_ps, tanh_done, gate_done, hidden_done = (
            sem(n) for n in ("ffn_ps", "tanh_done", "gate_done", "hidden_done"))
        ct_ps, ct_hi_done, ct_lo_done, attn_ps, attn_done = (
            sem(n) for n in ("ct_ps", "ct_hi_done", "ct_lo_done", "attn_ps", "attn_done"))
        had_ps, g_hi_done, g_lo_done, g_stored, g_in = (
            sem(n) for n in ("had_ps", "g_hi_done", "g_lo_done", "g_stored", "g_in"))
        h_hi_done = [sem(f"h_hi_done{i}") for i in range(2)]
        h_lo_done = [sem(f"h_lo_done{i}") for i in range(2)]
        h_used = [sem(f"h_used{i}") for i in range(2)]
        silu_t, silu_s = sem("silu_t"), sem("silu_s")
        silu_a = [sem(f"silu_a{i}") for i in range(2)]
        x_again = [sem(f"x_again{i}") for i in range(2)]
        y_done = [sem(f"y_done{i}") for i in range(2)]
        y_stored = [sem(f"y_stored{i}") for i in range(2)]

        block = ctx.enter_context(nc.Block())

        NQ, NO = 3 * KT, KT

        def stage_no(b, i):
            return b * (NQ + NO + JT) + i

        def split_no(b, i):
            return b * (NQ + NO) + i

        def stage_count(k):
            return (k // 3 + 1) * 16

        def begin_at_one(e, *counters):
            for s in counters:
                e.sem_inc(s, 1)

        ENGINES = 5

        def end_phase(e, n):
            e.drain().then_inc(phase_done, 1)
            e.wait_ge(phase_done, ENGINES * n)

        QK_GROUPS = [(c, m, o) for c in range(NC) for m in range(2) for o in range(KT)]
        NQK = len(QK_GROUPS)
        NG = NQK + NT
        PB = [F[0], F[1], O, X]

        def score_cols(c, k):
            need, end = max(c * W, k * P), (c + 1) * W
            return min(need, end - 2 * P), need, end

        def max_bank(t):
            return M[:].rearrange("p b w -> p (b w)") if t >= TPC else X[:, 0, :]

        def load_stack(sp, head, buf):
            for dst, at, which, part in ((q_st, 0, 0, 0), (q_st, 1, 0, 0), (q_st, 2, 0, 1),
                                         (k_st, 0, 1, 0), (k_st, 1, 1, 1), (k_st, 2, 1, 0)):
                sp.dma_start(dst[buf][at * DH:(at + 1) * DH, :].bitcast(F32),
                             qk_dram[which, part, bass.ds(head * DH, DH), :].bitcast(F32)
                             ).then_inc(stack_in[buf], 16)

        @block.sync
        def _(sp):
            begin_at_one(sp, m_in, *y_stored)
            sp.dma_start(had[:], hadamard).then_inc(had_in, 16)

            def project(b):
                xv = x[b].rearrange("(t p) d -> p t d", p=P)

                def load_weight(i):
                    if i >= 3:
                        sp.wait_ge(split_lo, split_no(b, i) - 2)
                    k = stage_no(b, i)
                    sp.dma_start(stage[k % 3][:], (wq, wk, wv)[i // KT][i % KT * P:(i % KT + 1) * P, :]
                                 ).then_inc(stage_in[k % 3], 16)

                for i in range(NT // 2):
                    sp.dma_start(xb[:, 2 * i:2 * i + 2, :], xv[:, 2 * i:2 * i + 2, :]
                                 ).then_inc(x_loaded[i], 16)
                    load_weight(i)
                for i in range(NT // 2, 2 * KT + 3):
                    load_weight(i)
                for g, (c, m, o) in enumerate(QK_GROUPS):
                    if g >= KT and 2 * KT + 3 + g - KT < NQ:
                        load_weight(2 * KT + 3 + g - KT)
                    sp.wait_ge(proj_lo_done, b * NG + g + 1)
                    for part, src in ((0, qk_hi), (1, qk_lo)):
                        sp.dma_start(qk_dram[m, part, o * P:(o + 1) * P, c * W:(c + 1) * W].bitcast(F32),
                                     src[g % 2][:].bitcast(F32)).then_inc(qk_stored[g % 2], 16)
                for i in range(2):
                    sp.wait_ge(qk_stored[i], (b + 1) * NQK // 2 * 32)

            def load_w13(j, n):
                sp.wait_ge(w13_lo_done, 1 + n)
                sp.dma_start(w13[:, 0, :], w1[bass.ds(j, 1)]).then_inc(w13_in, 16)
                sp.dma_start(w13[:, 1, :], w3[bass.ds(j, 1)]).then_inc(w13_in, 16)

            def store_maxima(n, buf):
                sp.wait_ge(m_lo_done, n + 1)
                for row, part in ((STACK, m_hi), (STACK + 1, m_lo)):
                    sp.dma_start(q_st[buf][row:row + 1, :].rearrange("o (t p) -> o t p", p=P).bitcast(F32),
                                 part[:].bitcast(F32)).then_inc(m_in, 16)

            def head_step(jj, u, n0):
                j = jj * 2 + u
                n = j + n0
                sp.wait_ge(scores_ps, 1 + n * NS)
                load_stack(sp, j + 1, 1 - u)
                load_w13(j + 1, n + 1)
                store_maxima(n + 1, 1 - u)

            def heads(b):
                n0 = b * NH
                load_stack(sp, 0, 0)
                load_w13(0, n0)
                store_maxima(n0, 0)
                with sp.Fori(0, NH // 2 - 1) as jj:
                    head_step(jj, 0, n0)
                    head_step(jj, 1, n0)
                head_step(NH // 2 - 1, 0, n0)

            def tail(b):
                for kt in range(NO):
                    i = NQ + kt
                    k = stage_no(b, i)
                    sp.wait_ge(split_lo, split_no(b, i) - 2)
                    sp.dma_start(stage[k % 3][:], wo[kt * P:(kt + 1) * P, :]).then_inc(stage_in[k % 3], 16)
                if b == 0:
                    for a in range(JT + 3):
                        if a < JT:
                            if a < 3:
                                sp.wait_ge(split_lo, split_no(0, NQ + NO) + a - 2)
                            else:
                                sp.wait_ge(had_ps, a - 2)
                            k = stage_no(0, NQ + NO) + a
                            sp.dma_start(stage[k % 3][:], w2b_dram[a]).then_inc(stage_in[k % 3], 16)
                        if a >= 3:
                            sp.wait_ge(g_lo_done, a - 2)
                            for part, src in ((0, g_hi), (1, g_lo)):
                                sp.dma_start(g_dram[part, :, a - 3, :].bitcast(F32),
                                             src[:, a - 3, :].bitcast(F32)).then_inc(g_stored, 16)
                else:
                    sp.wait_ge(g_stored, 2 * JT * 16)
                    for part, dst in ((0, g_hi), (1, g_lo)):
                        sp.dma_start(dst[:].bitcast(F32), g_dram[part].bitcast(F32)).then_inc(g_in, 16)

                def load_x(t, i):
                    sp.dma_start(x_in[i][:], x[b, bass.ds(t * P, P), :]).then_inc(x_again[i], 16)

                def store_y(tp, i):
                    sp.wait_ge(y_done[i], tp + (b * NT // 2 + 1))
                    sp.dma_start(out[b, bass.ds((tp * 2 + i) * P, P), :], y[i][:]).then_inc(y_stored[i], 16)

                load_x(0, 0)
                load_x(1, 1)
                with sp.Fori(0, NT // 2 - 1) as tp:
                    for i in range(2):
                        store_y(tp, i)
                        load_x(tp * 2 + (i + 2), i)
                for i in range(2):
                    store_y(NT // 2 - 1, i)
                for i in range(2):
                    sp.wait_ge(y_stored[i], 1 + (b + 1) * (NT // 2) * 16)

            for b in range(B):
                project(b)
                end_phase(sp, 3 * b + 1)
                heads(b)
                end_phase(sp, 3 * b + 2)
                tail(b)
                end_phase(sp, 3 * b + 3)

        @block.gpsimd
        def _(pool):
            begin_at_one(pool, w13_lo_done, ctx_done)
            pool.memset(ident[:], 0.0).then_inc(const_ready, 1)
            pool.memset(causal[:], 0.0).then_inc(const_ready, 1)
            pool.wait_ge(const_ready, 2)
            pool.affine_select(out=ident[:], in_=ident[:], compare_op=ALU.not_equal, fill=1.0, base=0,
                               pattern=[[-1, P]], channel_multiplier=1).then_inc(const_ready, 1)
            pool.affine_select(out=causal[:, S - P:S], in_=causal[:, S - P:S], compare_op=ALU.is_ge,
                               fill=MASKED, base=0, pattern=[[-1, P]], channel_multiplier=1
                               ).then_inc(const_ready, 1)

            def transform_w2():
                done = 0
                for s in range(D // P):
                    cols = slice(s * P, (s + 1) * P)
                    a = wht_in[s % 2]
                    if s == 0:
                        pool.dma_start(a[:], w2[:, :, cols].rearrange("a p d -> p a d")).then_inc(wht_loaded, 16)
                    pool.wait_ge(wht_loaded, (s + 1) * 16)
                    if s + 1 < D // P:
                        if s >= 1:
                            pool.wait_ge(wht_stored, s * 16)
                        pool.dma_start(wht_in[(s + 1) % 2][:],
                                       w2[:, :, (s + 1) * P:(s + 2) * P].rearrange("a p d -> p a d")
                                       ).then_inc(wht_loaded, 16)
                    src, dst = a, wht_mid
                    for st in range(4):
                        h = 1 << st
                        sv = src[:].rearrange("p (g two h) d -> p g two (h d)", two=2, h=h)
                        dv = dst[:].rearrange("p (g two h) d -> p g two (h d)", two=2, h=h)
                        for half, op in ((0, ALU.add), (1, ALU.subtract)):
                            pool.tensor_tensor(dv[:, :, half, :], sv[:, :, 0, :], sv[:, :, 1, :], op
                                               ).then_inc(wht_step, 1)
                        done += 2
                        pool.wait_ge(wht_step, done)
                        src, dst = dst, src
                    pool.dma_start(w2b_dram[:, :, cols].rearrange("a p d -> p a d"), a[:]
                                   ).then_inc(wht_stored, 16)
                pool.wait_ge(wht_stored, D // P * 16)

            def mask(n, s):
                pool.wait_ge(exp_done, 1 + n * NS + (s + 1))
                pool.sem_inc(mask_begun, 1)
                e = expd[s % 3][:, 0:P]
                pool.affine_select(out=e, in_=e, compare_op=ALU.is_ge, fill=0.0, base=0, pattern=[[1, P]],
                                   channel_multiplier=-1).then_inc(mask_done, 1)

            def prepare(j, n, buf):
                pool.wait_ge(w13_hi_done, n + 1)
                pool.tensor_tensor(w13_lo[buf][:], w13[:], w13_hi[buf][:].bitcast(F32), ALU.subtract
                                   ).then_inc(w13_lo_done, 1)
                pool.tensor_copy(vh[buf][:].bitcast(F32), vparts[:, :, bass.ds(j, 1), :].bitcast(F32)
                                 ).then_inc(vh_ready, 1)

            def scale_ctx(j, n, c):
                pool.wait_ge(o_read, 1 + n * 2 + (c + 1))
                pool.tensor_tensor(ctx_nat[:, c * TPC:(c + 1) * TPC, bass.ds(j * DH, DH)], ctx_raw[c][:],
                                   rden[c][:].unsqueeze(2).broadcast_to([P, TPC, DH]), ALU.mult
                                   ).then_inc(ctx_done, 1)

            def head_step(jj, u, n0, last=False):
                j = jj * 2 + u
                n = j + n0
                for s in range(TPC):
                    mask(n, s)
                if not last:
                    pool.wait_ge(pv_done, 1 + n * NS)
                    prepare(j + 1, n + 1, 1 - u)
                scale_ctx(j, n, 0)
                for s in range(NS - TPC, NS):
                    mask(n, s)
                scale_ctx(j, n, 1)

            def heads(b):
                n0 = b * NH
                prepare(0, n0, 0)
                with pool.Fori(0, NH // 2 - 1) as jj:
                    head_step(jj, 0, n0)
                    head_step(jj, 1, n0)
                head_step(NH // 2 - 1, 0, n0)
                head_step(NH // 2 - 1, 1, n0, last=True)

            for b in range(B):
                pool.memset(vparts[:, :, :, VS:VC], 1.0).then_inc(ones_ready, 1)
                if b == 0:
                    transform_w2()
                end_phase(pool, 3 * b + 1)
                heads(b)
                end_phase(pool, 3 * b + 2)
                end_phase(pool, 3 * b + 3)

        @block.scalar
        def _(act):
            begin_at_one(act, exp_done)
            def split_weight(b, i):
                k = stage_no(b, i)
                act.wait_ge(stage_in[k % 3], stage_count(k))
                dst = wo_hi if i >= NQ else w_hi[i // KT]
                act.activation(dst[:, i % KT, :], stage[k % 3][:], ACT.Copy).then_inc(split_hi, 1)

            def project(b):
                for i in range(KT):
                    split_weight(b, i)
                act.wait_ge(var_done, b + 1)
                act.activation(std[:], var[:], ACT.Sqrt).then_inc(sqrt_done, 1)

                def xt(t):
                    act.wait_ge(xt_ps, b * NT + t + 1)
                    act.activation(xt_hi[:, :, t * P:(t + 1) * P],
                                   SB[t % 2][:, 0, :].rearrange("p (k c) -> p k c", k=KT), ACT.Copy
                                   ).then_inc(xt_hi_done, 1)

                def qk(g):
                    act.wait_ge(proj_ps, b * NG + g + 1)
                    if b > 0 or g >= 2:
                        act.wait_ge(qk_stored[g % 2], (b * NQK + g) // 2 * 32)
                    act.activation(qk_hi[g % 2][:], PB[g % 4][:, 0, :], ACT.Copy,
                                   scale=SCALE if QK_GROUPS[g][1] == 0 else 1.0).then_inc(proj_hi_done, 1)

                for t in range(TPC):
                    xt(t)
                for i in range(KT, 2 * KT):
                    split_weight(b, i)
                for t in range(TPC, NT):
                    xt(t)
                    qk(t - TPC)
                for i in range(2 * KT, 3 * KT):
                    split_weight(b, i)
                for g in range(TPC, NQK):
                    qk(g)
                for t in range(NT + 1):
                    if t < NT:
                        g = NQK + t
                        act.wait_ge(proj_ps, b * NG + g + 1)
                        act.activation(vparts[:, t, :, 2 * DH:3 * DH],
                                       PB[g % 4][:, 0, :].rearrange("p (h d) -> p h d", h=NH), ACT.Copy
                                       ).then_inc(proj_hi_done, 1)
                    if t >= 1:
                        act.wait_ge(proj_lo_done, b * NG + NQK + t)
                        act.activation(vparts[:, t - 1, :, DH:2 * DH],
                                       vrest[(t - 1) % 2][:].rearrange("p (h d) -> p h d", h=NH), ACT.Copy
                                       ).then_inc(v2_done, 1)

            def exp(n, s):
                c, k = STEPS[s]
                start, need, end = score_cols(c, k)
                act.wait_ge(scores_ps, 1 + n * NS + (s + 1))
                act.wait_ge(p_lo_done, 1 + n * NS + max(s - 2, 0))
                act.activation(expd[s % 3][:, 0:end - need], SB[s % 2][:, 0, need - start:end - start],
                               ACT.Exp).then_inc(exp_done, 1)

            def probs_hi(n, s):
                c, k = STEPS[s]
                _, need, end = score_cols(c, k)
                act.wait_ge(exp_done, 1 + n * NS + (s + 1))
                if k * P >= c * W:
                    act.wait_ge(mask_done, n * NT + (k + 1))
                act.wait_ge(pv_done, 1 + n * NS + max(s - 2, 0))
                act.activation(p_hi[s % 3][:, 0:end - need], expd[s % 3][:, 0:end - need], ACT.Copy
                               ).then_inc(p_hi_done, 1)

            def tanh(n, c):
                act.wait_ge(ffn_ps, 1 + n * GROUPS + (2 * c + 1))
                act.wait_ge(gate_done, 1 + n * 2 + c)
                act.activation(gate_t[:], F[0][:, 0, :], ACT.Tanh, scale=0.5).then_inc(tanh_done, 1)

            def maxima_hi(n):
                act.wait_ge(mt_ps, n + 1)
                act.wait_ge(m_in, 1 + n * 32)
                act.activation(m_hi[:], X[0:NT, 0, 0:P], ACT.Copy, scale=-1.0).then_inc(m_hi_done, 1)

            def head_step(jj, u, n0, last=False):
                n = jj * 2 + (u + n0)
                for s in range(NS + 1):
                    if s < NS:
                        exp(n, s)
                    if s >= 1:
                        probs_hi(n, s - 1)
                    if s in TANH_AT:
                        tanh(n, TANH_AT[s])
                if not last:
                    maxima_hi(n + 1)

            def heads(b):
                n0 = b * NH
                maxima_hi(n0)
                with act.Fori(0, NH // 2 - 1) as jj:
                    head_step(jj, 0, n0)
                    head_step(jj, 1, n0)
                head_step(NH // 2 - 1, 0, n0)
                head_step(NH // 2 - 1, 1, n0, last=True)

            def tail(b):
                for i in range(NQ, NQ + NO):
                    split_weight(b, i)
                for t in range(NT + 1):
                    if t < NT:
                        act.wait_ge(ct_ps, b * NT + t + 1)
                        if t >= 2:
                            act.wait_ge(attn_ps, b * NT + t - 1)
                        act.activation(ct_hi[t % 2][:], SB[t % 2][:, 0, :].rearrange("p (k c) -> p k c", k=KT),
                                       ACT.Copy).then_inc(ct_hi_done, 1)
                        if b == 0:
                            for a in (2 * t, 2 * t + 1):
                                act.wait_ge(had_ps, a + 1)
                                act.activation(g_hi[:, a, :], F[a % 2][:, 0, :], ACT.Copy, scale=W2_SCALE
                                               ).then_inc(g_hi_done, 1)
                    if t >= 1:
                        act.wait_ge(attn_ps, b * NT + t)
                        act.activation(ctx_nat[:, t - 1, :], M[:, (t - 1) % 2, :], ACT.Copy
                                       ).then_inc(attn_done, 1)

                def hidden_hi(t):
                    for i in range(2):
                        act.wait_ge(h_used[i], 1 + t + b * NT)
                        act.activation(h_hi[i][:], hidden[:, i * (JT // 2):(i + 1) * (JT // 2), bass.ds(t * P, P)],
                                       ACT.Copy).then_inc(h_hi_done[i], 1)

                def gate(tp, i):
                    act.wait_ge(h_used[1], 1 + tp * 2 + (i + 1 + b * NT))
                    act.wait_ge(y_stored[i], 1 + (tp + b * NT // 2) * 16)
                    act.activation(y[i][:], F[i][:, 0, :], ACT.Tanh, scale=0.5).then_inc(silu_t, 1)

                hidden_hi(0)
                with act.Fori(0, NT // 2 - 1) as tp:
                    for i in range(2):
                        hidden_hi(tp * 2 + (i + 1))
                        gate(tp, i)
                hidden_hi(NT - 1)
                gate(NT // 2 - 1, 0)
                gate(NT // 2 - 1, 1)

            for b in range(B):
                project(b)
                end_phase(act, 3 * b + 1)
                heads(b)
                end_phase(act, 3 * b + 2)
                tail(b)
                end_phase(act, 3 * b + 3)

        @block.vector
        def _(dve):
            begin_at_one(dve, p_lo_done, gate_done, hidden_done, o_read, max_done, *silu_a)
            def split_weight(b, i):
                k = stage_no(b, i)
                dve.wait_ge(split_hi, split_no(b, i) + 1)
                hi, lo = (wo_hi, wo_lo) if i >= NQ else (w_hi[i // KT], w_lo[i // KT])
                dve.tensor_tensor(lo[:, i % KT, :], stage[k % 3][:], hi[:, i % KT, :].bitcast(F32), ALU.subtract
                                  ).then_inc(split_lo, 1)

            def project(b):
                for t in range(NT):
                    if t % 2 == 0:
                        dve.wait_ge(x_loaded[t // 2], (b + 1) * 16)
                    dve.bn_stats(stats[:, t, :], xb[:, t, :]).then_inc(stats_done, 1)
                    if t % 2 == 1:
                        split_weight(b, t // 2)
                for t in range(NT):
                    dve.wait_ge(stats_done, b * NT + t + 1)
                    dve.bn_aggr(mv[:, t, :], stats[:, t, :]).then_inc(mv_done, 1)
                dve.wait_ge(mv_done, (b + 1) * NT)
                dve.tensor_scalar(var[:], mv[:, :, 1], EPS, None, ALU.add).then_inc(var_done, 1)
                dve.wait_ge(sqrt_done, b + 1)
                dve.reciprocal(tmp[:], std[:]).then_inc(newton, 1)
                dve.wait_ge(newton, 5 * b + 1)
                dve.tensor_tensor(tmp[:], tmp[:], var[:], ALU.mult).then_inc(newton, 1)
                dve.wait_ge(newton, 5 * b + 2)
                dve.tensor_tensor(tmp[:], tmp[:], std[:], ALU.add).then_inc(newton, 1)
                dve.wait_ge(newton, 5 * b + 3)
                dve.tensor_scalar(tmp[:], tmp[:], 0.5, None, ALU.mult).then_inc(newton, 1)
                dve.wait_ge(newton, 5 * b + 4)
                dve.reciprocal(rstd[:], tmp[:]).then_inc(newton, 1)
                dve.wait_ge(newton, 5 * b + 5)

                def xn(t):
                    dve.tensor_scalar(xb[:, t, :], xb[:, t, :], mv[:, t, 0:1], rstd[:, t:t + 1],
                                      ALU.subtract, ALU.mult).then_inc(xn_done, 1)

                def xt(t):
                    dve.wait_ge(xt_hi_done, b * NT + t + 1)
                    at = (slice(None), slice(None), slice(t * P, (t + 1) * P))
                    dve.tensor_tensor(xt_lo[at], SB[t % 2][:, 0, :].rearrange("p (k c) -> p k c", k=KT),
                                      xt_hi[at].bitcast(F32), ALU.subtract).then_inc(xt_lo_done, 1)

                def qk(g):
                    dve.wait_ge(proj_hi_done, b * NG + g + 1)
                    ps, hi = PB[g % 4][:, 0, :], qk_hi[g % 2][:].bitcast(F32)
                    dve.scalar_tensor_tensor(qk_lo[g % 2][:], ps, SCALE if QK_GROUPS[g][1] == 0 else 1.0, hi,
                                             ALU.mult, ALU.subtract).then_inc(proj_lo_done, 1)

                xn(0)
                for t in range(TPC):
                    if t + 1 < TPC:
                        xn(t + 1)
                    xt(t)
                for t in range(TPC, NT):
                    xn(t)
                for i in range(KT, 2 * KT):
                    split_weight(b, i)
                for t in range(TPC, NT):
                    xt(t)
                    qk(t - TPC)
                for i in range(2 * KT, 3 * KT):
                    split_weight(b, i)
                for g in range(TPC, NQK):
                    qk(g)
                for t in range(NT + 1):
                    heads_of = lambda v: v.rearrange("p (h d) -> p h d", h=NH)
                    if t < NT:
                        g = NQK + t
                        dve.wait_ge(proj_hi_done, b * NG + g + 1)
                        if t >= 2:
                            dve.wait_ge(v3_done, b * NT + t - 1)
                        dve.tensor_tensor(heads_of(vrest[t % 2][:]), heads_of(PB[g % 4][:, 0, :]),
                                          vparts[:, t, :, 2 * DH:3 * DH], ALU.subtract
                                          ).then_inc(proj_lo_done, 1)
                    if t >= 1:
                        dve.wait_ge(v2_done, b * NT + t)
                        dve.tensor_tensor(vparts[:, t - 1, :, 0:DH], heads_of(vrest[(t - 1) % 2][:]),
                                          vparts[:, t - 1, :, DH:2 * DH], ALU.subtract).then_inc(v3_done, 1)

            def maxima(n, buf, r):
                t = MAX_ORDER[r]
                width = (t + 1) * P
                dve.wait_ge(max_ps, n * NT + (r + 1))
                dve.sem_inc(max_begun, 1)
                dve.tensor_tensor_reduce(out=unused[r % 2][:, 0:width], in0=max_bank(t)[:, 0:width],
                                         in1=causal[:, S - width:S], scale=1.0, scalar=0.0, op0=ALU.add,
                                         op1=ALU.max, accum_out=mx[:, t:t + 1]).then_inc(max_done, 1)

            def maxima_lo(n):
                dve.wait_ge(m_hi_done, n + 1)
                dve.scalar_tensor_tensor(m_lo[:], X[0:NT, 0, 0:P], -1.0, m_hi[:].bitcast(F32), ALU.mult,
                                         ALU.subtract).then_inc(m_lo_done, 1)

            def w13_high(n, buf):
                dve.wait_ge(w13_in, (n + 1) * 32)
                dve.tensor_copy(w13_hi[buf][:], w13[:]).then_inc(w13_hi_done, 1)

            def probs_lo(n, s):
                c, k = STEPS[s]
                _, need, end = score_cols(c, k)
                dve.wait_ge(p_hi_done, n * NS + (s + 1))
                dve.tensor_tensor(p_lo[s % 3][:, 0:end - need], expd[s % 3][:, 0:end - need],
                                  p_hi[s % 3][:, 0:end - need], ALU.subtract).then_inc(p_lo_done, 1)

            def read_ctx(n, c):
                dve.wait_ge(pv_done, 1 + n * NS + (TPC if c == 0 else NS))
                dve.wait_ge(ctx_done, 1 + n * 2)
                o = O[:, 0, 0:TPC * VC].rearrange("p (t v) -> p t v", v=VC)
                dve.reciprocal(rden[c][:], o[:, :, VS])
                dve.tensor_reduce(ctx_raw[c][:], o[:, :, 0:VS].rearrange("p t (a d) -> p t d a", a=3),
                                  op=ALU.add, axis=AX.X).then_inc(o_read, 1)

            def gate(n, c):
                dve.wait_ge(tanh_done, n * 2 + (c + 1))
                dve.wait_ge(hidden_done, 1 + n * 2 + c)
                dve.scalar_tensor_tensor(gate_a[:], gate_t[:], 1.0, F[0][:, 0, :], ALU.add, ALU.mult
                                         ).then_inc(gate_done, 1)

            def hide(j, n, c):
                dve.wait_ge(gate_done, 1 + n * 2 + (c + 1))
                dve.wait_ge(ffn_ps, 1 + n * GROUPS + (2 * c + 2))
                dve.tensor_tensor(hidden[:, bass.ds(j, 1), c * W:(c + 1) * W], gate_a[:].unsqueeze(1),
                                  F[1][:], ALU.mult).then_inc(hidden_done, 1)

            def head_step(jj, u, n0, last=False):
                j = jj * 2 + u
                n = j + n0
                for s in range(1, NS + 1):
                    probs_lo(n, s - 1)
                    if s == 5:
                        read_ctx(n, 0)
                    if not last and s == 3:
                        dve.wait_ge(ffn_ps, 1 + n * GROUPS)
                        w13_high(n + 1, 1 - u)
                    if not last and MAX_SLOT <= s < MAX_SLOT + NT:
                        maxima(n + 1, 1 - u, s - MAX_SLOT)
                    if s == 6:
                        gate(n, 0)
                    if s == 8:
                        hide(j, n, 0)
                if not last:
                    maxima_lo(n + 1)
                gate(n, 1)
                read_ctx(n, 1)
                hide(j, n, 1)

            def heads(b):
                n0 = b * NH
                w13_high(n0, 0)
                for i in range(2):
                    dve.memset(k_st[i][STACK:STACK + 2, :].bitcast(F32), 1.0).then_inc(ones_ready, 1)
                for r in range(NT):
                    maxima(n0, 0, r)
                maxima_lo(n0)
                with dve.Fori(0, NH // 2 - 1) as jj:
                    head_step(jj, 0, n0)
                    head_step(jj, 1, n0)
                head_step(NH // 2 - 1, 0, n0)
                head_step(NH // 2 - 1, 1, n0, last=True)

            def tail(b):
                for i in range(NQ, NQ + NO):
                    split_weight(b, i)
                for t in range(NT):
                    dve.wait_ge(ct_hi_done, b * NT + t + 1)
                    dve.tensor_tensor(ct_lo[t % 2][:], SB[t % 2][:, 0, :].rearrange("p (k c) -> p k c", k=KT),
                                      ct_hi[t % 2][:].bitcast(F32), ALU.subtract).then_inc(ct_lo_done, 1)
                    if b == 0:
                        for a in (2 * t, 2 * t + 1):
                            dve.wait_ge(g_hi_done, a + 1)
                            dve.scalar_tensor_tensor(g_lo[:, a, :], F[a % 2][:, 0, :], W2_SCALE,
                                                     g_hi[:, a, :].bitcast(F32), ALU.mult, ALU.subtract
                                                     ).then_inc(g_lo_done, 1)

                def hidden_lo(t):
                    for i in range(2):
                        dve.wait_ge(h_hi_done[i], t + (b * NT + 1))
                        dve.tensor_tensor(h_lo[i][:],
                                          hidden[:, i * (JT // 2):(i + 1) * (JT // 2), bass.ds(t * P, P)],
                                          h_hi[i][:].bitcast(F32), ALU.subtract).then_inc(h_lo_done[i], 1)

                def finish(tp, i):
                    t = tp * 2 + i
                    dve.wait_ge(silu_t, t + (b * NT + 1))
                    dve.scalar_tensor_tensor(y[i][:], y[i][:], 1.0, F[i][:, 0, :], ALU.add, ALU.mult
                                             ).then_inc(silu_a[i], 1)
                    dve.wait_ge(silu_a[i], 1 + tp + (b * NT // 2 + 1))
                    dve.tensor_tensor(y[i][:].unsqueeze(1), y[i][:].unsqueeze(1), ctx_nat[:, bass.ds(t, 1), :],
                                      ALU.mult).then_inc(silu_s, 1)
                    dve.wait_ge(silu_s, t + (b * NT + 1))
                    dve.wait_ge(x_again[i], (tp + (b * NT // 2 + 1)) * 16)
                    dve.scalar_tensor_tensor(y[i][:], y[i][:], 0.5, x_in[i][:], ALU.mult, ALU.add
                                             ).then_inc(y_done[i], 1)

                dve.wait_ge(attn_done, (b + 1) * NT)
                hidden_lo(0)
                with dve.Fori(0, NT // 2 - 1) as tp:
                    for i in range(2):
                        hidden_lo(tp * 2 + (i + 1))
                        finish(tp, i)
                hidden_lo(NT - 1)
                finish(NT // 2 - 1, 0)
                finish(NT // 2 - 1, 1)

            dve.wait_ge(const_ready, 4)
            for b in range(B):
                project(b)
                end_phase(dve, 3 * b + 1)
                heads(b)
                end_phase(dve, 3 * b + 2)
                tail(b)
                end_phase(dve, 3 * b + 3)

        @block.tensor
        def _(pe):
            begin_at_one(pe, scores_ps, pv_done, ffn_ps, *h_used)
            def three(o, a_hi, a_lo, b_hi, b_lo, first, last):
                pe.matmul(o, a_hi, b_hi, start=first, stop=False)
                pe.matmul(o, a_hi, b_lo, start=False, stop=False)
                return pe.matmul(o, a_lo, b_hi, start=False, stop=last)

            def project(b):
                def transpose(t):
                    pe.wait_ge(xn_done, b * NT + t + 1)
                    if t >= 2:
                        pe.wait_ge(xt_lo_done, b * NT + t - 1)
                    for kt in range(KT):
                        mm = pe.transpose(SB[t % 2][:, 0, kt * P:(kt + 1) * P], xb[:, t, kt * P:(kt + 1) * P],
                                          ident[:])
                    mm.then_inc(xt_ps, 1)

                def group(g):
                    if g >= 4:
                        pe.wait_ge(proj_lo_done, b * NG + g - 3)
                    o = PB[g % 4][:, 0, :]
                    if g < NQK:
                        c, m, r = QK_GROUPS[g]
                        pe.wait_ge(xt_lo_done, b * NT + (c + 1) * TPC)
                        pe.wait_ge(split_lo, split_no(b, (m + 1) * KT))
                    else:
                        t, m = g - NQK, 2
                        pe.wait_ge(split_lo, split_no(b, NQ))
                    for kt in range(KT):
                        if g < NQK:
                            a = [w[m][:, kt, r * P:(r + 1) * P] for w in (w_hi, w_lo)]
                            v = [xt[:, kt, c * W:(c + 1) * W] for xt in (xt_hi, xt_lo)]
                        else:
                            a = [xt[:, kt, t * P:(t + 1) * P] for xt in (xt_hi, xt_lo)]
                            v = [w[m][:, kt, :] for w in (w_hi, w_lo)]
                        mm = three(o, *a, *v, kt == 0, kt == KT - 1)
                    mm.then_inc(proj_ps, 1)

                for t in range(TPC):
                    transpose(t)
                for t in range(TPC, NT):
                    group(t - TPC)
                    transpose(t)
                for g in range(TPC, NG):
                    group(g)

            def maxima(n, buf, r):
                t = MAX_ORDER[r]
                end = (t + 1) * P
                if r >= 2:
                    pe.wait_ge(max_done, 1 + n * NT + (r - 1))
                for at in range(0, end, W):
                    width = min(W, max(end - at, 2 * P))
                    mm = pe.matmul(max_bank(t)[:, at:at + width], q_st[buf][0:STACK, t * P:(t + 1) * P],
                                   k_st[buf][0:STACK, at:at + width], start=True, stop=True)
                mm.then_inc(max_ps, 1)

            def transpose_maxima(n):
                pe.wait_ge(max_done, 1 + (n + 1) * NT)
                pe.transpose(X[0:NT, 0, 0:P], mx[:], ident[:]).then_inc(mt_ps, 1)

            def scores(n, buf, s):
                c, k = STEPS[s]
                start, _, end = score_cols(c, k)
                pe.wait_ge(exp_done, 1 + n * NS + max(s - 1, 0))
                pe.matmul(SB[s % 2][:, 0, 0:end - start], k_st[buf][0:STACK + 2, k * P:(k + 1) * P],
                          q_st[buf][0:STACK + 2, start:end], start=True, stop=True).then_inc(scores_ps, 1)

            def context(n, buf, s):
                c, k = STEPS[s]
                _, need, end = score_cols(c, k)
                if k == 0:
                    pe.wait_ge(o_read, 1 + n * 2 + c)
                pe.wait_ge(p_lo_done, 1 + n * NS + (s + 1))
                for t in range(need // P, end // P):
                    at = t * P - need
                    o = (t - c * TPC) * VC
                    last = t == k
                    pe.matmul(O[:, 0, o:o + VC], p_hi[s % 3][:, at:at + P], vh[buf][:, k, :],
                              start=k == 0 and t == c * TPC, stop=False, skip_group_check=True)
                    mm = pe.matmul(O[:, 0, o + DH:o + VC], p_lo[s % 3][:, at:at + P], vh[buf][:, k, DH:VC],
                                   start=False, stop=last, skip_group_check=True)
                mm.then_inc(pv_done, 1)

            def ffn(n, buf, first, end):
                for i in range(first, end):
                    g, k = divmod(i, GMM)
                    c, m = divmod(g, 2)
                    kt, p = divmod(k, 3)
                    if i == 0:
                        pe.wait_ge(w13_lo_done, 1 + n + 1)
                    if k == 0:
                        pe.wait_ge(hidden_done if m else gate_done, 1 + n * 2 + c)
                    w = (w13_hi, w13_hi, w13_lo)[p][buf][:, m, kt * P:(kt + 1) * P]
                    v = (xt_hi, xt_lo, xt_hi)[p][:, kt, c * W:(c + 1) * W]
                    mm = pe.matmul(F[m][:, 0, :], w, v, start=k == 0, stop=k == GMM - 1)
                    if k == GMM - 1:
                        mm.then_inc(ffn_ps, 1)

            def head_step(jj, u, n0, last=False):
                n = jj * 2 + (u + n0)
                done = 0
                for s in range(NS + 2):
                    if s == 0:
                        ffn(n, u, 0, FFN_UPTO[0])
                        pe.wait_ge(m_in, 1 + (n + 1) * 32)
                        pe.wait_ge(vh_ready, n + 1)
                    if s < NS:
                        scores(n, u, s)
                    if s > 0:
                        ffn(n, u, done, FFN_UPTO[s])
                    done = FFN_UPTO[s]
                    if not last and MAX_SLOT <= s < MAX_SLOT + NT:
                        if s == MAX_SLOT:
                            pe.wait_ge(stack_in[1 - u], (jj + (n0 // 2 + 1 + u)) * 96)
                        maxima(n + 1, 1 - u, s - MAX_SLOT)
                    if not last and s == NS:
                        transpose_maxima(n + 1)
                    if s >= 2:
                        context(n, u, s - 2)

            def heads(b):
                n0 = b * NH
                pe.wait_ge(ones_ready, 3 * (b + 1))
                pe.wait_ge(stack_in[0], (n0 // 2 + 1) * 96)
                for r in range(NT):
                    maxima(n0, 0, r)
                transpose_maxima(n0)
                with pe.Fori(0, NH // 2 - 1) as jj:
                    head_step(jj, 0, n0)
                    head_step(jj, 1, n0)
                head_step(NH // 2 - 1, 0, n0)
                head_step(NH // 2 - 1, 1, n0, last=True)

            def tail(b):
                def transpose(t):
                    if t >= 2:
                        pe.wait_ge(ct_lo_done, b * NT + t - 1)
                    for kt in range(KT):
                        mm = pe.transpose(SB[t % 2][:, 0, kt * P:(kt + 1) * P],
                                          ctx_nat[:, t, kt * P:(kt + 1) * P], ident[:])
                    mm.then_inc(ct_ps, 1)

                def hadamard_128(a):
                    k = stage_no(0, NQ + NO) + a
                    pe.wait_ge(stage_in[k % 3], stage_count(k))
                    if a >= 2:
                        pe.wait_ge(g_lo_done, a - 1)
                    pe.matmul(F[a % 2][:, 0, :], had[:], stage[k % 3][:], start=True, stop=True
                              ).then_inc(had_ps, 1)

                def attention_out(t):
                    pe.wait_ge(ct_lo_done, b * NT + t + 1)
                    if t >= 2:
                        pe.wait_ge(attn_done, b * NT + t - 1)
                    for kt in range(KT):
                        mm = three(M[:, t % 2, :], ct_hi[t % 2][:, kt, :], ct_lo[t % 2][:, kt, :],
                                   wo_hi[:, kt, :], wo_lo[:, kt, :], kt == 0, kt == KT - 1)
                    mm.then_inc(attn_ps, 1)

                transpose(0)
                pe.wait_ge(split_lo, split_no(b, NQ + NO))
                for t in range(NT):
                    if t + 1 < NT:
                        transpose(t + 1)
                    if b == 0:
                        hadamard_128(2 * t)
                        hadamard_128(2 * t + 1)
                    attention_out(t)

                def down(tp, i):
                    t = tp * 2 + i
                    pe.wait_ge(silu_a[i], 1 + tp + b * NT // 2)
                    for h in range(2):
                        pe.wait_ge(h_lo_done[h], t + (b * NT + 1))
                        for k in range(JT // 2):
                            j = h * (JT // 2) + k
                            mm = three(F[i][:, 0, :], h_hi[h][:, k, :], h_lo[h][:, k, :], g_hi[:, j, :],
                                       g_lo[:, j, :], j == 0, j == JT - 1)
                        mm.then_inc(h_used[h], 1)

                if b == 0:
                    pe.wait_ge(g_lo_done, JT)
                else:
                    pe.wait_ge(g_in, 32)
                with pe.Fori(0, NT // 2) as tp:
                    for i in range(2):
                        down(tp, i)

            pe.wait_ge(const_ready, 4)
            pe.wait_ge(had_in, 16)
            for b in range(B):
                project(b)
                end_phase(pe, 3 * b + 1)
                heads(b)
                end_phase(pe, 3 * b + 2)
                tail(b)
                end_phase(pe, 3 * b + 3)


def kernel(L0_attn_x, L0_attn_Wq, L0_attn_Wk, L0_attn_Wv, L0_attn_Wo, L0_ffn_W1, L0_ffn_W2, L0_ffn_W3):
    import numpy as np
    import concourse.bacc as bacc
    from concourse.bass_utils import run_bass_kernel_spmd

    def tiles(w):
        w = np.asarray(w).reshape(JT, P, KT, P)
        return np.ascontiguousarray(w.transpose(0, 3, 2, 1)).reshape(JT, P, D)

    sylvester = np.ones((1, 1), np.float32)
    while sylvester.shape[0] < P:
        sylvester = np.block([[sylvester, sylvester], [sylvester, -sylvester]])
    arrays = {
        "x": np.ascontiguousarray(L0_attn_x),
        "wq": np.ascontiguousarray(np.asarray(L0_attn_Wq).T),
        "wk": np.ascontiguousarray(np.asarray(L0_attn_Wk).T),
        "wv": np.ascontiguousarray(np.asarray(L0_attn_Wv).T),
        "wo": np.ascontiguousarray(np.asarray(L0_attn_Wo).T),
        "w1": tiles(L0_ffn_W1),
        "w3": tiles(L0_ffn_W3),
        "w2": np.ascontiguousarray(np.asarray(L0_ffn_W2).T).reshape(JT, P, D),
        "hadamard": np.ascontiguousarray(sylvester),
    }
    nc = bacc.Bacc("TRN2", target_bir_lowering=False, num_devices=1)
    args = [nc.dram_tensor(n, a.shape, mybir.dt.from_np(a.dtype), kind="ExternalInput").ap()
            for n, a in arrays.items()]
    out = nc.dram_tensor("out", (B, S, D), F32, kind="ExternalOutput").ap()
    build(nc, *args, out)
    r = run_bass_kernel_spmd(nc, [arrays], core_ids=[0])
    return r.results[0]["out"]
```

```python
import concourse.bass as bass
from concourse import mybir
from contextlib import ExitStack

F32 = mybir.dt.float32
F32R = mybir.dt.float32r
F16 = mybir.dt.float16
BF16 = mybir.dt.bfloat16
ALU = mybir.AluOpType
ACT = mybir.ActivationFunctionType
AX = mybir.AxisListType

P = 128
B, S, D = 2, 1024, 512
HID = 2048
NH, DH = 16, 32
KT = D // P
JT = HID // P
NT = S // P
W = 512
NC = S // W
TPC = W // P
SCALE = float(DH) ** -0.5
EPS = 1e-5
W2_SCALE = 0.5 * float(HID) ** -0.5
MASKED = -1e38
VC = 98
VS = 3 * DH
STACK = 3 * DH
STEPS = [(c, k) for c in range(NC) for k in range(TPC * (c + 1))]
NS = len(STEPS)
MAX_ORDER = [7, 0, 6, 1, 5, 2, 4, 3]
LAG = 3
NP = LAG + 1
POOL_LO = [5, 7]
DVE_LO = [s for s in range(NS) if s not in POOL_LO]
MAX_SLOT = 3
MT_SLOT = 11
MAX_TILE = 4
GROUPS = 4
GMM = 3 * KT
FFN_UPTO = [8, 11, 14, 17, 19, 21, 23, 26, 28, 30, 33, 37, 41, 45, 48]
HIDE_SLOT = 8
GATE_AT = {4: 0, 12: 1}
TANH_AT = {3: 0, 12: 1}


def build(nc, x, wq, wk, wv, wo, w1w3, w2, hadamard, out):
    stacks = nc.dram_tensor("qk_stacks", [2, 3, D, S], F32R, kind="Internal").ap()
    w2b_dram = nc.dram_tensor("w2_butterflied", [JT, P, D], F32, kind="Internal").ap()
    g_dram = nc.dram_tensor("w2_transformed", [2, P, JT, D], F32R, kind="Internal").ap()

    ctx = ExitStack()
    with ctx:
        def sb(name, shape, dt, stack=ctx):
            return stack.enter_context(nc.sbuf_tensor(name, shape, dt))

        def bank(name, banks=1):
            return ctx.enter_context(nc.psum_tensor(name, [P, banks, W], F32))

        def sem(name):
            return ctx.enter_context(nc.semaphore(name))

        ident = sb("ident", [P, P], F32)
        had = sb("had", [P, P], F32)
        causal = sb("causal", [P, S], BF16)
        ctx_nat = sb("ctx_nat", [P, NT, D], F32)
        stage = [sb(f"stage{i}", [P, D], F32) for i in range(3)]
        stats = sb("stats", [P, NT, 6], F32)
        mv = sb("mv", [P, NT, 2], F32)
        var, std, rstd, tmp = (sb(n, [P, NT], F32) for n in ("var", "std", "rstd", "tmp"))

        with ExitStack() as r:
            hidden = sb("hidden", [P, JT, S], F32, r)
        w_hi = [sb(f"w{m}_hi", [P, KT, D], F32R) for m in range(3)]
        w_lo = [sb(f"w{m}_lo", [P, KT, D], F32R) for m in range(3)]
        wht_in = [sb(f"wht_in{i}", [P, JT, P], F32) for i in range(2)]

        with ExitStack() as r:
            xb = sb("xb", [P, NT, D], F32, r)
        with ExitStack() as r:
            q_st = [sb(f"q_st{i}", [P, S], F32R, r) for i in range(2)]
            k_st = [sb(f"k_st{i}", [P, S], F32R, r) for i in range(2)]
        wo_hi = sb("wo_hi", [P, KT, D], F32R)
        wo_lo = sb("wo_lo", [P, KT, D], F32R)

        with ExitStack() as r:
            xt_hi = sb("xt_hi", [P, KT, S], F32R, r)
            xt_lo = sb("xt_lo", [P, KT, S], F32R, r)
            vparts = sb("vparts", [P, NT, NH, VC], BF16, r)
            mx = sb("mx", [P, NT], F32, r)
            m_hi = sb("m_hi", [NT, P], F32R, r)
            m_lo = sb("m_lo", [NT, P], F32R, r)
            w13 = sb("w13", [P, 2, D], F32, r)
            w13_hi0 = sb("w13_hi0", [P, 2, D], F32R, r)
            w13_lo0 = sb("w13_lo0", [P, 2, D], F32R, r)
            with ExitStack() as q:
                wht_mid = sb("wht_mid", [P, JT, P], F32, q)
                qk_hi = [sb(f"qk_hi{i}", [P, W], F32R, q) for i in range(2)]
                qk_lo = [sb(f"qk_lo{i}", [P, W], F32R, q) for i in range(2)]
                vrest = [sb(f"vrest{i}", [P, W], F32, q) for i in range(2)]
            w13_hi = [w13_hi0, sb("w13_hi1", [P, 2, D], F32R, r)]
            w13_lo = [w13_lo0, sb("w13_lo1", [P, 2, D], F32R, r)]
            expd = [sb(f"expd{i}", [P, W], F32, r) for i in range(NP)]
            p_hi = [sb(f"p_hi{i}", [P, W], F16, r) for i in range(NP)]
            p_lo = [sb(f"p_lo{i}", [P, W], F16, r) for i in range(NP)]
            gate_t = sb("gate_t", [P, W], F32, r)
            gate_a = sb("gate_a", [P, W], F32, r)
            vh = [sb(f"vh{i}", [P, NT, VC], BF16, r) for i in range(2)]
            ctx_raw = [sb(f"ctx_raw{i}", [P, TPC, DH], F32, r) for i in range(NC)]
            rden = [sb(f"rden{i}", [P, TPC], F32, r) for i in range(NC)]
        g_hi = sb("g_hi", [P, JT, D], F32R)
        g_lo = sb("g_lo", [P, JT, D], F32R)
        h_hi = [sb(f"h_hi{i}", [P, JT // 2, P], F32R) for i in range(2)]
        h_lo = [sb(f"h_lo{i}", [P, JT // 2, P], F32R) for i in range(2)]
        ct_hi = [sb(f"ct_hi{i}", [P, KT, P], F32R) for i in range(2)]
        ct_lo = [sb(f"ct_lo{i}", [P, KT, P], F32R) for i in range(2)]
        x_in = [sb(f"x_in{i}", [P, D], F32) for i in range(2)]
        y = [sb(f"y{i}", [P, D], F32) for i in range(2)]

        F = [bank("f0"), bank("f1")]
        SB = [bank("s0"), bank("s1")]
        M = bank("m", 2)
        X = bank("xs")
        O = bank("o")

        const_ready = sem("const_ready")
        had_in = sem("had_in")
        phase_done = sem("phase_done")
        x_loaded = [sem(f"x_loaded{i}") for i in range(NT // 2)]
        stage_in = [sem(f"stage_in{i}") for i in range(3)]
        split_hi, split_lo = sem("split_hi"), sem("split_lo")
        stats_done, mv_done, var_done, sqrt_done, newton = (
            sem(n) for n in ("stats_done", "mv_done", "var_done", "sqrt_done", "newton"))
        xn_done, xt_ps, xt_hi_done, xt_lo_done = (
            sem(n) for n in ("xn_done", "xt_ps", "xt_hi_done", "xt_lo_done"))
        proj_ps, proj_hi_done, proj_lo_done = (sem(n) for n in ("proj_ps", "proj_hi_done", "proj_lo_done"))
        v2_done, v3_done = sem("v2_done"), sem("v3_done")
        qk_stored = [sem(f"qk_stored{i}") for i in range(2)]
        wht_loaded, wht_step, wht_stored = sem("wht_loaded"), sem("wht_step"), sem("wht_stored")
        ones_ready = sem("ones_ready")
        stack_in = [sem(f"stack_in{i}") for i in range(2)]
        max_ps, max_done, mt_ps, m_hi_done, m_lo_done, m_in = (
            sem(n) for n in ("max_ps", "max_done", "mt_ps", "m_hi_done", "m_lo_done", "m_in"))
        scores_ps, exp_done, mask_done, p_hi_done, p_lo_done, p_lo_pool, pv_done = (
            sem(n) for n in ("scores_ps", "exp_done", "mask_done", "p_hi_done", "p_lo_done", "p_lo_pool", "pv_done"))
        max_begun, mask_begun = sem("max_begun"), sem("mask_begun")
        o_read, ctx_done, vh_ready = sem("o_read"), sem("ctx_done"), sem("vh_ready")
        w13_in, w13_hi_done, w13_lo_done = sem("w13_in"), sem("w13_hi_done"), sem("w13_lo_done")
        ffn_ps, tanh_done, gate_done, hidden_done = (
            sem(n) for n in ("ffn_ps", "tanh_done", "gate_done", "hidden_done"))
        ct_ps, ct_hi_done, ct_lo_done, attn_ps, attn_done = (
            sem(n) for n in ("ct_ps", "ct_hi_done", "ct_lo_done", "attn_ps", "attn_done"))
        had_ps, g_hi_done, g_lo_done, g_stored, g_in = (
            sem(n) for n in ("had_ps", "g_hi_done", "g_lo_done", "g_stored", "g_in"))
        h_hi_done = [sem(f"h_hi_done{i}") for i in range(2)]
        h_lo_done = [sem(f"h_lo_done{i}") for i in range(2)]
        h_used = [sem(f"h_used{i}") for i in range(2)]
        silu_t, silu_s = sem("silu_t"), sem("silu_s")
        silu_a = [sem(f"silu_a{i}") for i in range(2)]
        x_again = [sem(f"x_again{i}") for i in range(2)]
        y_done = [sem(f"y_done{i}") for i in range(2)]
        y_stored = [sem(f"y_stored{i}") for i in range(2)]

        block = ctx.enter_context(nc.Block())

        NQ, NO = 3 * KT, KT

        def stage_no(b, i):
            return b * (NQ + NO + JT) + i

        def split_no(b, i):
            return b * (NQ + NO) + i

        def stage_count(k):
            return (k // 3 + 1) * 16

        def begin_at_one(e, *counters):
            for s in counters:
                e.sem_inc(s, 1)

        ENGINES = 5

        def end_phase(e, n):
            e.drain().then_inc(phase_done, 1)
            e.wait_ge(phase_done, ENGINES * n)

        QK_GROUPS = [(c, m, o) for c in range(NC) for m in range(2) for o in range(KT)]
        NQK = len(QK_GROUPS)
        NG = NQK + NT

        def group_bank(g):
            return (F[0], F[1], O, X if g < NQK else SB[0])[g % 4][:, 0, :]

        def score_cols(c, k):
            need, end = max(c * W, k * P), (c + 1) * W
            return min(need, end - 2 * P), need, end

        def max_bank(t):
            return M[:].rearrange("p b w -> p (b w)") if t >= TPC else X[:, 0, :]

        class Head:

            def __init__(self, jj, m):
                self.jj, self.m, self.buf = jj, m, m % 2

            def next(self):
                return Head(self.jj, self.m + 1)

            def count(self, each, more=0):
                return self.jj * (2 * each) + (self.m * each + more + 1)

            def count0(self, each, more):
                return self.jj * (2 * each) + (self.m * each + more)

        def wait_lo(e, h, s):
            if s in POOL_LO:
                e.wait_ge(p_lo_pool, h.count(len(POOL_LO), POOL_LO.index(s) + 1))
            else:
                e.wait_ge(p_lo_done, h.count(len(DVE_LO), DVE_LO.index(s) + 1))

        def load_stack(sp, head, buf):
            for which, dst in enumerate((q_st, k_st)):
                sp.dma_start(dst[buf][0:STACK, :].bitcast(F32),
                             stacks[which, :, bass.ds(head * DH, DH), :].bitcast(F32)
                             ).then_inc(stack_in[buf], 16)

        @block.sync
        def _(sp):
            begin_at_one(sp, m_in, *y_stored)

            def load_weight(b, i):
                if i >= 3:
                    sp.wait_ge(split_lo, split_no(b, i) - 2)
                k = stage_no(b, i)
                sp.dma_start(stage[k % 3][:], (wq, wk, wv, wo)[i // KT][i % KT * P:(i % KT + 1) * P, :]
                             ).then_inc(stage_in[k % 3], 16)

            def load_first(b):
                xv = x[b].rearrange("(t p) d -> p t d", p=P)

                def load_pair(i):
                    sp.dma_start(xb[:, 2 * i:2 * i + 2, :], xv[:, 2 * i:2 * i + 2, :]
                                 ).then_inc(x_loaded[i], 16)

                load_pair(0)
                load_pair(1)
                for i in range(3):
                    load_weight(b, i)
                load_pair(2)
                load_pair(3)

            def project(b):
                for i in range(3, 2 * KT + 3):
                    load_weight(b, i)
                for g, (c, m, o) in enumerate(QK_GROUPS):
                    if g >= KT and 2 * KT + 3 + g - KT < NQ:
                        load_weight(b, 2 * KT + 3 + g - KT)
                    sp.wait_ge(proj_lo_done, b * NG + g + 1)
                    for part, src in enumerate((qk_hi, qk_lo, qk_hi) if m else (qk_hi, qk_hi, qk_lo)):
                        sp.dma_start(stacks[m, part, o * P:(o + 1) * P, c * W:(c + 1) * W].bitcast(F32),
                                     src[g % 2][:].bitcast(F32)).then_inc(qk_stored[g % 2], 16)
                for i in range(2):
                    sp.wait_ge(qk_stored[i], (b + 1) * NQK // 2 * 48)
                load_stack(sp, 0, 0)
                load_w13(0, Head(0, b * NH))
                for i in range(NQ, NQ + 3):
                    load_weight(b, i)
                store_maxima(Head(0, b * NH))

            def load_w13(j, h):
                sp.wait_ge(w13_lo_done, h.count(1))
                sp.dma_start(w13[:], w1w3[bass.ds(j, 1)]).then_inc(w13_in, 16)

            def store_maxima(h):
                sp.wait_ge(m_lo_done, h.count0(1, 1))
                for row, part in ((STACK, m_hi), (STACK + 1, m_lo)):
                    sp.dma_start(q_st[h.buf][row:row + 1, :].rearrange("o (t p) -> o t p", p=P).bitcast(F32),
                                 part[:].bitcast(F32)).then_inc(m_in, 16)

            def head_step(jj, u, n0, last=False):
                j, h = jj * 2 + u, Head(jj, n0 + u)
                sp.wait_ge(scores_ps, h.count(NS))
                load_stack(sp, j + 1, 1 - u)
                if not last:
                    load_w13(j + 2, h.next().next())
                store_maxima(h.next())

            def heads(b):
                n0 = b * NH
                load_w13(1, Head(0, n0 + 1))
                with sp.Fori(0, NH // 2 - 1) as jj:
                    head_step(jj, 0, n0)
                    head_step(jj, 1, n0)
                head_step(NH // 2 - 1, 0, n0, last=True)

            def tail(b):
                for i in range(NQ + 3, NQ + NO):
                    load_weight(b, i)
                if b == 0:
                    for a in range(JT + 3):
                        if a < JT:
                            if a < 3:
                                sp.wait_ge(split_lo, split_no(0, NQ + NO) + a - 2)
                            else:
                                sp.wait_ge(had_ps, a - 2)
                            k = stage_no(0, NQ + NO) + a
                            sp.dma_start(stage[k % 3][:], w2b_dram[a]).then_inc(stage_in[k % 3], 16)
                        if a >= 3:
                            sp.wait_ge(g_lo_done, a - 2)
                            for part, src in ((0, g_hi), (1, g_lo)):
                                sp.dma_start(g_dram[part, :, a - 3, :].bitcast(F32),
                                             src[:, a - 3, :].bitcast(F32)).then_inc(g_stored, 16)
                else:
                    sp.wait_ge(g_stored, 2 * JT * 16)
                    for part, dst in ((0, g_hi), (1, g_lo)):
                        sp.dma_start(dst[:].bitcast(F32), g_dram[part].bitcast(F32)).then_inc(g_in, 16)

                def load_x(t, i):
                    sp.dma_start(x_in[i][:], x[b, bass.ds(t * P, P), :]).then_inc(x_again[i], 16)

                def store_y(tp, i):
                    sp.wait_ge(y_done[i], tp + (b * NT // 2 + 1))
                    sp.dma_start(out[b, bass.ds((tp * 2 + i) * P, P), :], y[i][:]).then_inc(y_stored[i], 16)

                load_x(0, 0)
                load_x(1, 1)
                if b + 1 < B:
                    sp.wait_ge(attn_ps, (b + 1) * NT)
                    load_first(b + 1)
                with sp.Fori(0, NT // 2 - 1) as tp:
                    for i in range(2):
                        store_y(tp, i)
                        load_x(tp * 2 + (i + 2), i)
                for i in range(2):
                    store_y(NT // 2 - 1, i)
                for i in range(2):
                    sp.wait_ge(y_stored[i], 1 + (b + 1) * (NT // 2) * 16)

            load_first(0)
            sp.dma_start(had[:], hadamard).then_inc(had_in, 16)
            for b in range(B):
                project(b)
                end_phase(sp, 3 * b + 1)
                heads(b)
                end_phase(sp, 3 * b + 2)
                tail(b)
                end_phase(sp, 3 * b + 3)

        @block.gpsimd
        def _(pool):
            begin_at_one(pool, w13_lo_done, p_lo_pool, ctx_done)
            pool.memset(ident[:], 0.0).then_inc(const_ready, 1)
            pool.memset(causal[:], 0.0).then_inc(const_ready, 1)
            pool.wait_ge(const_ready, 2)
            pool.affine_select(out=ident[:], in_=ident[:], compare_op=ALU.not_equal, fill=1.0, base=0,
                               pattern=[[-1, P]], channel_multiplier=1).then_inc(const_ready, 1)
            pool.affine_select(out=causal[:, S - P:S], in_=causal[:, S - P:S], compare_op=ALU.is_ge,
                               fill=MASKED, base=0, pattern=[[-1, P]], channel_multiplier=1
                               ).then_inc(const_ready, 1)

            def transform_w2():
                done = 0
                for s in range(D // P):
                    cols = slice(s * P, (s + 1) * P)
                    a = wht_in[s % 2]
                    if s == 0:
                        pool.dma_start(a[:], w2[:, :, cols].rearrange("a p d -> p a d")).then_inc(wht_loaded, 16)
                    pool.wait_ge(wht_loaded, (s + 1) * 16)
                    if s + 1 < D // P:
                        if s >= 1:
                            pool.wait_ge(wht_stored, s * 16)
                        pool.dma_start(wht_in[(s + 1) % 2][:],
                                       w2[:, :, (s + 1) * P:(s + 2) * P].rearrange("a p d -> p a d")
                                       ).then_inc(wht_loaded, 16)
                    src, dst = a, wht_mid
                    for st in range(4):
                        h = 1 << st
                        sv = src[:].rearrange("p (g two h) d -> p g two (h d)", two=2, h=h)
                        dv = dst[:].rearrange("p (g two h) d -> p g two (h d)", two=2, h=h)
                        for half, op in ((0, ALU.add), (1, ALU.subtract)):
                            pool.tensor_tensor(dv[:, :, half, :], sv[:, :, 0, :], sv[:, :, 1, :], op
                                               ).then_inc(wht_step, 1)
                        done += 2
                        pool.wait_ge(wht_step, done)
                        src, dst = dst, src
                    pool.dma_start(w2b_dram[:, :, cols].rearrange("a p d -> p a d"), a[:]
                                   ).then_inc(wht_stored, 16)
                pool.wait_ge(wht_stored, D // P * 16)

            def mask(h, s):
                pool.wait_ge(exp_done, h.count(NS, s + 1))
                pool.sem_inc(mask_begun, 1)
                e = expd[s % NP][:, 0:P]
                pool.affine_select(out=e, in_=e, compare_op=ALU.is_ge, fill=0.0, base=0, pattern=[[1, P]],
                                   channel_multiplier=-1).then_inc(mask_done, 1)

            def w13_low(h):
                pool.wait_ge(w13_hi_done, h.count0(1, 1))
                pool.tensor_tensor(w13_lo[h.buf][:], w13[:], w13_hi[h.buf][:].bitcast(F32), ALU.subtract
                                   ).then_inc(w13_lo_done, 1)

            def head_v(j, h):
                pool.tensor_copy(vh[h.buf][:].bitcast(F32), vparts[:, :, bass.ds(j, 1), :].bitcast(F32)
                                 ).then_inc(vh_ready, 1)

            def probs_lo(h, s):
                c, k = STEPS[s]
                _, need, end = score_cols(c, k)
                pool.wait_ge(p_hi_done, h.count0(NS, s + 1))
                pool.tensor_tensor(p_lo[s % NP][:, 0:end - need], expd[s % NP][:, 0:end - need],
                                   p_hi[s % NP][:, 0:end - need], ALU.subtract).then_inc(p_lo_pool, 1)

            def scale_ctx(j, h, c):
                pool.wait_ge(o_read, h.count(NC, c + 1))
                pool.tensor_tensor(ctx_nat[:, c * TPC:(c + 1) * TPC, bass.ds(j * DH, DH)], ctx_raw[c][:],
                                   rden[c][:].unsqueeze(2).broadcast_to([P, TPC, DH]), ALU.mult
                                   ).then_inc(ctx_done, 1)

            def head_step(jj, u, n0, last=False):
                j, h = jj * 2 + u, Head(jj, n0 + u)
                for s in range(TPC):
                    mask(h, s)
                if not last:
                    w13_low(h.next())
                    pool.wait_ge(pv_done, h.count(NS))
                    head_v(j + 1, h.next())
                for s in range(TPC, NS):
                    if s in POOL_LO:
                        probs_lo(h, s)
                    if s == TPC + LAG:
                        scale_ctx(j, h, 0)
                    if STEPS[s][1] >= TPC:
                        mask(h, s)
                scale_ctx(j, h, 1)

            def heads(b):
                n0 = b * NH
                head_v(0, Head(0, n0))
                with pool.Fori(0, NH // 2 - 1) as jj:
                    head_step(jj, 0, n0)
                    head_step(jj, 1, n0)
                head_step(NH // 2 - 1, 0, n0)
                head_step(NH // 2 - 1, 1, n0, last=True)

            for b in range(B):
                pool.memset(vparts[:, :, :, VS:VC], 1.0).then_inc(ones_ready, 1)
                if b == 0:
                    transform_w2()
                w13_low(Head(0, b * NH))
                end_phase(pool, 3 * b + 1)
                heads(b)
                end_phase(pool, 3 * b + 2)
                end_phase(pool, 3 * b + 3)

        @block.scalar
        def _(act):
            begin_at_one(act, exp_done)
            def split_weight(b, i):
                k = stage_no(b, i)
                act.wait_ge(stage_in[k % 3], stage_count(k))
                dst = wo_hi if i >= NQ else w_hi[i // KT]
                act.activation(dst[:, i % KT, :], stage[k % 3][:], ACT.Copy).then_inc(split_hi, 1)

            def root(b, half):
                c = slice(half * TPC, (half + 1) * TPC)
                act.wait_ge(var_done, 2 * b + half + 1)
                act.activation(std[:, c], var[:, c], ACT.Sqrt).then_inc(sqrt_done, 1)

            def project(b):
                def xt(t):
                    act.wait_ge(xt_ps, b * NT + t + 1)
                    act.activation(xt_hi[:, :, t * P:(t + 1) * P],
                                   SB[t % 2][:, 0, :].rearrange("p (k c) -> p k c", k=KT), ACT.Copy
                                   ).then_inc(xt_hi_done, 1)

                def qk(g):
                    act.wait_ge(proj_ps, b * NG + g + 1)
                    if b > 0 or g >= 2:
                        act.wait_ge(qk_stored[g % 2], (b * NQK + g) // 2 * 48)
                    act.activation(qk_hi[g % 2][:], group_bank(g), ACT.Copy,
                                   scale=SCALE if QK_GROUPS[g][1] == 0 else 1.0).then_inc(proj_hi_done, 1)

                if b == 0:
                    root(b, 0)
                for i in range(3):
                    split_weight(b, i)
                for t in range(TPC):
                    xt(t)
                split_weight(b, 3)
                if b == 0:
                    root(b, 1)
                for i in range(KT, 2 * KT):
                    split_weight(b, i)
                for t in range(TPC, NT):
                    xt(t)
                    qk(t - TPC)
                for i in range(2 * KT, 3 * KT):
                    split_weight(b, i)
                for g in range(TPC, NQK):
                    qk(g)
                for t in range(NT + 1):
                    if t == NT - 1:
                        w13_high(Head(0, b * NH))
                    if t < NT:
                        g = NQK + t
                        act.wait_ge(proj_ps, b * NG + g + 1)
                        act.activation(vparts[:, t, :, 2 * DH:3 * DH],
                                       group_bank(g).rearrange("p (h d) -> p h d", h=NH), ACT.Copy
                                       ).then_inc(proj_hi_done, 1)
                    if t >= 1:
                        act.wait_ge(proj_lo_done, b * NG + NQK + t)
                        act.activation(vparts[:, t - 1, :, DH:2 * DH],
                                       vrest[(t - 1) % 2][:].rearrange("p (h d) -> p h d", h=NH), ACT.Copy
                                       ).then_inc(v2_done, 1)
                maxima_hi(Head(0, b * NH))

            def exp(h, s):
                c, k = STEPS[s]
                start, need, end = score_cols(c, k)
                act.wait_ge(scores_ps, h.count(NS, s + 1))
                if s >= NP:
                    wait_lo(act, h, s - NP)
                elif s == 0:
                    act.wait_ge(p_lo_done, h.count(len(DVE_LO)))
                    act.wait_ge(p_lo_pool, h.count(len(POOL_LO)))
                act.activation(expd[s % NP][:, 0:end - need], SB[s % 2][:, 0, need - start:end - start],
                               ACT.Exp).then_inc(exp_done, 1)

            def probs_hi(h, s):
                c, k = STEPS[s]
                _, need, end = score_cols(c, k)
                act.wait_ge(exp_done, h.count(NS, s + 1))
                if k * P >= c * W:
                    act.wait_ge(mask_done, h.count0(NT, k + 1))
                act.wait_ge(pv_done, h.count(NS, max(s - NP + 1, 0)))
                act.activation(p_hi[s % NP][:, 0:end - need], expd[s % NP][:, 0:end - need], ACT.Copy
                               ).then_inc(p_hi_done, 1)

            def tanh(h, c):
                act.wait_ge(ffn_ps, h.count(GROUPS, 2 * c + 1))
                act.wait_ge(gate_done, h.count(NC, c))
                act.activation(gate_t[:], F[0][:, 0, :], ACT.Tanh, scale=0.5).then_inc(tanh_done, 1)

            def w13_high(h):
                act.wait_ge(w13_in, h.count0(16, 16))
                act.activation(w13_hi[h.buf][:], w13[:], ACT.Copy).then_inc(w13_hi_done, 1)

            def maxima_hi(h):
                act.wait_ge(mt_ps, h.count0(1, 1))
                act.wait_ge(m_in, h.count(32))
                act.activation(m_hi[:], X[0:NT, 0, 0:P], ACT.Copy, scale=-1.0).then_inc(m_hi_done, 1)

            def head_step(jj, u, n0, last=False):
                h = Head(jj, n0 + u)
                if not last:
                    act.wait_ge(ffn_ps, h.count(GROUPS))
                    w13_high(h.next())
                for s in range(NS + 1):
                    if s < NS:
                        exp(h, s)
                    if s >= 1:
                        probs_hi(h, s - 1)
                    if s in TANH_AT:
                        tanh(h, TANH_AT[s])
                    if not last and s == MT_SLOT + 1:
                        maxima_hi(h.next())

            def heads(b):
                n0 = b * NH
                act.preload_act_table(ACT.Exp)
                with act.Fori(0, NH // 2 - 1) as jj:
                    head_step(jj, 0, n0)
                    head_step(jj, 1, n0)
                head_step(NH // 2 - 1, 0, n0)
                head_step(NH // 2 - 1, 1, n0, last=True)

            def tail(b):
                for i in range(NQ, NQ + NO):
                    split_weight(b, i)
                for t in range(NT + 1):
                    if t < NT:
                        act.wait_ge(ct_ps, b * NT + t + 1)
                        if t >= 2:
                            act.wait_ge(attn_ps, b * NT + t - 1)
                        act.activation(ct_hi[t % 2][:], SB[t % 2][:, 0, :].rearrange("p (k c) -> p k c", k=KT),
                                       ACT.Copy).then_inc(ct_hi_done, 1)
                        if b == 0:
                            for a in (2 * t, 2 * t + 1):
                                act.wait_ge(had_ps, a + 1)
                                act.activation(g_hi[:, a, :], F[a % 2][:, 0, :], ACT.Copy, scale=W2_SCALE
                                               ).then_inc(g_hi_done, 1)
                    if t >= 1:
                        act.wait_ge(attn_ps, b * NT + t)
                        act.activation(ctx_nat[:, t - 1, :], M[:, (t - 1) % 2, :], ACT.Copy
                                       ).then_inc(attn_done, 1)

                def hidden_hi(t):
                    for i in range(2):
                        act.wait_ge(h_used[i], 1 + t + b * NT)
                        act.activation(h_hi[i][:], hidden[:, i * (JT // 2):(i + 1) * (JT // 2), bass.ds(t * P, P)],
                                       ACT.Copy).then_inc(h_hi_done[i], 1)

                def gate(tp, i):
                    act.wait_ge(h_used[1], 1 + tp * 2 + (i + 1 + b * NT))
                    act.wait_ge(y_stored[i], 1 + (tp + b * NT // 2) * 16)
                    act.activation(y[i][:], F[i][:, 0, :], ACT.Tanh, scale=0.5).then_inc(silu_t, 1)

                hidden_hi(0)
                with act.Fori(0, NT // 2 - 1) as tp:
                    for i in range(2):
                        hidden_hi(tp * 2 + (i + 1))
                        gate(tp, i)
                if b + 1 < B:
                    root(b + 1, 0)
                hidden_hi(NT - 1)
                if b + 1 < B:
                    root(b + 1, 1)
                gate(NT // 2 - 1, 0)
                gate(NT // 2 - 1, 1)

            for b in range(B):
                project(b)
                end_phase(act, 3 * b + 1)
                heads(b)
                end_phase(act, 3 * b + 2)
                tail(b)
                end_phase(act, 3 * b + 3)

        @block.vector
        def _(dve):
            begin_at_one(dve, p_lo_done, gate_done, hidden_done, o_read, max_done, *silu_a)
            def split_weight(b, i):
                k = stage_no(b, i)
                dve.wait_ge(split_hi, split_no(b, i) + 1)
                hi, lo = (wo_hi, wo_lo) if i >= NQ else (w_hi[i // KT], w_lo[i // KT])
                dve.tensor_tensor(lo[:, i % KT, :], stage[k % 3][:], hi[:, i % KT, :].bitcast(F32), ALU.subtract
                                  ).then_inc(split_lo, 1)

            def normalise(b, half):
                tiles, c = range(half * TPC, (half + 1) * TPC), slice(half * TPC, (half + 1) * TPC)
                n = 2 * b + half
                for t in tiles:
                    if t % 2 == 0:
                        dve.wait_ge(x_loaded[t // 2], (b + 1) * 16)
                    dve.bn_stats(stats[:, t, :], xb[:, t, :]).then_inc(stats_done, 1)
                for t in tiles:
                    dve.wait_ge(stats_done, b * NT + t + 1)
                    dve.bn_aggr(mv[:, t, :], stats[:, t, :]).then_inc(mv_done, 1)
                dve.wait_ge(mv_done, (n + 1) * TPC)
                dve.tensor_scalar(var[:, c], mv[:, c, 1], EPS, None, ALU.add).then_inc(var_done, 1)
                dve.wait_ge(sqrt_done, n + 1)
                dve.reciprocal(tmp[:, c], std[:, c]).then_inc(newton, 1)
                dve.wait_ge(newton, 5 * n + 1)
                dve.tensor_tensor(tmp[:, c], tmp[:, c], var[:, c], ALU.mult).then_inc(newton, 1)
                dve.wait_ge(newton, 5 * n + 2)
                dve.tensor_tensor(tmp[:, c], tmp[:, c], std[:, c], ALU.add).then_inc(newton, 1)
                dve.wait_ge(newton, 5 * n + 3)
                dve.tensor_scalar(tmp[:, c], tmp[:, c], 0.5, None, ALU.mult).then_inc(newton, 1)
                dve.wait_ge(newton, 5 * n + 4)
                dve.reciprocal(rstd[:, c], tmp[:, c]).then_inc(newton, 1)
                dve.wait_ge(newton, 5 * n + 5)
                for t in tiles:
                    dve.tensor_scalar(xb[:, t, :], xb[:, t, :], mv[:, t, 0:1], rstd[:, t:t + 1],
                                      ALU.subtract, ALU.mult).then_inc(xn_done, 1)

            def project(b):
                def xt(t):
                    dve.wait_ge(xt_hi_done, b * NT + t + 1)
                    at = (slice(None), slice(None), slice(t * P, (t + 1) * P))
                    dve.tensor_tensor(xt_lo[at], SB[t % 2][:, 0, :].rearrange("p (k c) -> p k c", k=KT),
                                      xt_hi[at].bitcast(F32), ALU.subtract).then_inc(xt_lo_done, 1)

                def qk(g):
                    dve.wait_ge(proj_hi_done, b * NG + g + 1)
                    ps, hi = group_bank(g), qk_hi[g % 2][:].bitcast(F32)
                    dve.scalar_tensor_tensor(qk_lo[g % 2][:], ps, SCALE if QK_GROUPS[g][1] == 0 else 1.0, hi,
                                             ALU.mult, ALU.subtract).then_inc(proj_lo_done, 1)

                if b == 0:
                    normalise(b, 0)
                for i in range(3):
                    split_weight(b, i)
                for t in range(TPC):
                    xt(t)
                split_weight(b, 3)
                if b == 0:
                    normalise(b, 1)
                for i in range(KT, 2 * KT):
                    split_weight(b, i)
                for t in range(TPC, NT):
                    xt(t)
                    qk(t - TPC)
                for i in range(2 * KT, 3 * KT):
                    split_weight(b, i)
                for i in range(2):
                    dve.memset(k_st[i][STACK:STACK + 2, :].bitcast(F32), 1.0).then_inc(ones_ready, 1)
                for g in range(TPC, NQK):
                    qk(g)
                for t in range(NT + 1):
                    heads_of = lambda v: v.rearrange("p (h d) -> p h d", h=NH)
                    if t < NT:
                        g = NQK + t
                        dve.wait_ge(proj_hi_done, b * NG + g + 1)
                        if t >= 2:
                            dve.wait_ge(v3_done, b * NT + t - 1)
                        dve.tensor_tensor(heads_of(vrest[t % 2][:]), heads_of(group_bank(g)),
                                          vparts[:, t, :, 2 * DH:3 * DH], ALU.subtract
                                          ).then_inc(proj_lo_done, 1)
                    if t >= 1:
                        dve.wait_ge(v2_done, b * NT + t)
                        dve.tensor_tensor(vparts[:, t - 1, :, 0:DH], heads_of(vrest[(t - 1) % 2][:]),
                                          vparts[:, t - 1, :, DH:2 * DH], ALU.subtract).then_inc(v3_done, 1)
                    if MAX_TILE <= t < NT:
                        for r in range(2 * (t - MAX_TILE), 2 * (t - MAX_TILE) + 2):
                            maxima(Head(0, b * NH), r)
                maxima_lo(Head(0, b * NH))

            def maxima(h, r):
                t = MAX_ORDER[r]
                width = (t + 1) * P
                dve.wait_ge(max_ps, h.count0(NT, r + 1))
                dve.sem_inc(max_begun, 1)
                dve.tensor_tensor_reduce(out=max_bank(t)[:, 0:width], in0=max_bank(t)[:, 0:width],
                                         in1=causal[:, S - width:S], scale=1.0, scalar=0.0, op0=ALU.add,
                                         op1=ALU.max, accum_out=mx[:, t:t + 1]).then_inc(max_done, 1)

            def maxima_lo(h):
                dve.wait_ge(m_hi_done, h.count0(1, 1))
                dve.scalar_tensor_tensor(m_lo[:], X[0:NT, 0, 0:P], -1.0, m_hi[:].bitcast(F32), ALU.mult,
                                         ALU.subtract).then_inc(m_lo_done, 1)

            def probs_lo(h, s):
                c, k = STEPS[s]
                _, need, end = score_cols(c, k)
                dve.wait_ge(p_hi_done, h.count0(NS, s + 1))
                dve.tensor_tensor(p_lo[s % NP][:, 0:end - need], expd[s % NP][:, 0:end - need],
                                  p_hi[s % NP][:, 0:end - need], ALU.subtract).then_inc(p_lo_done, 1)

            def read_ctx(h, c):
                dve.wait_ge(pv_done, h.count(NS, TPC if c == 0 else NS))
                dve.wait_ge(ctx_done, h.count(NC))
                o = O[:, 0, 0:TPC * VC].rearrange("p (t v) -> p t v", v=VC)
                dve.reciprocal(rden[c][:], o[:, :, VS])
                dve.tensor_reduce(ctx_raw[c][:], o[:, :, 0:VS].rearrange("p t (a d) -> p t d a", a=3),
                                  op=ALU.add, axis=AX.X).then_inc(o_read, 1)

            def gate(h, c):
                dve.wait_ge(tanh_done, h.count0(NC, c + 1))
                dve.wait_ge(hidden_done, h.count(NC, c))
                dve.scalar_tensor_tensor(gate_a[:], gate_t[:], 1.0, F[0][:, 0, :], ALU.add, ALU.mult
                                         ).then_inc(gate_done, 1)

            def hide(j, h, c):
                dve.wait_ge(gate_done, h.count(NC, c + 1))
                dve.wait_ge(ffn_ps, h.count(GROUPS, 2 * c + 2))
                dve.tensor_tensor(hidden[:, bass.ds(j, 1), c * W:(c + 1) * W], gate_a[:].unsqueeze(1),
                                  F[1][:], ALU.mult).then_inc(hidden_done, 1)

            def head_step(jj, u, n0, last=False):
                j, h = jj * 2 + u, Head(jj, n0 + u)
                for s in range(1, NS + 1):
                    if s == TPC + LAG - 1:
                        read_ctx(h, 0)
                    if not last and MAX_SLOT <= s < MAX_SLOT + NT:
                        maxima(h.next(), s - MAX_SLOT)
                    if s - 1 in DVE_LO:
                        probs_lo(h, s - 1)
                    if s in GATE_AT:
                        gate(h, GATE_AT[s])
                    if s == HIDE_SLOT:
                        hide(j, h, 0)
                    if not last and s == MT_SLOT + 1:
                        maxima_lo(h.next())
                read_ctx(h, 1)
                hide(j, h, 1)

            def heads(b):
                n0 = b * NH
                with dve.Fori(0, NH // 2 - 1) as jj:
                    head_step(jj, 0, n0)
                    head_step(jj, 1, n0)
                head_step(NH // 2 - 1, 0, n0)
                head_step(NH // 2 - 1, 1, n0, last=True)

            def tail(b):
                for i in range(NQ, NQ + NO):
                    split_weight(b, i)
                for t in range(NT):
                    dve.wait_ge(ct_hi_done, b * NT + t + 1)
                    dve.tensor_tensor(ct_lo[t % 2][:], SB[t % 2][:, 0, :].rearrange("p (k c) -> p k c", k=KT),
                                      ct_hi[t % 2][:].bitcast(F32), ALU.subtract).then_inc(ct_lo_done, 1)
                    if b == 0:
                        for a in (2 * t, 2 * t + 1):
                            dve.wait_ge(g_hi_done, a + 1)
                            dve.scalar_tensor_tensor(g_lo[:, a, :], F[a % 2][:, 0, :], W2_SCALE,
                                                     g_hi[:, a, :].bitcast(F32), ALU.mult, ALU.subtract
                                                     ).then_inc(g_lo_done, 1)

                def hidden_lo(t):
                    for i in range(2):
                        dve.wait_ge(h_hi_done[i], t + (b * NT + 1))
                        dve.tensor_tensor(h_lo[i][:],
                                          hidden[:, i * (JT // 2):(i + 1) * (JT // 2), bass.ds(t * P, P)],
                                          h_hi[i][:].bitcast(F32), ALU.subtract).then_inc(h_lo_done[i], 1)

                def finish(tp, i):
                    t = tp * 2 + i
                    dve.wait_ge(silu_t, t + (b * NT + 1))
                    dve.scalar_tensor_tensor(y[i][:], y[i][:], 1.0, F[i][:, 0, :], ALU.add, ALU.mult
                                             ).then_inc(silu_a[i], 1)
                    dve.wait_ge(silu_a[i], 1 + tp + (b * NT // 2 + 1))
                    dve.tensor_tensor(y[i][:].unsqueeze(1), y[i][:].unsqueeze(1), ctx_nat[:, bass.ds(t, 1), :],
                                      ALU.mult).then_inc(silu_s, 1)
                    dve.wait_ge(silu_s, t + (b * NT + 1))
                    dve.wait_ge(x_again[i], (tp + (b * NT // 2 + 1)) * 16)
                    dve.scalar_tensor_tensor(y[i][:], y[i][:], 0.5, x_in[i][:], ALU.mult, ALU.add
                                             ).then_inc(y_done[i], 1)

                dve.wait_ge(attn_done, (b + 1) * NT)
                hidden_lo(0)
                with dve.Fori(0, NT // 2 - 1) as tp:
                    for i in range(2):
                        hidden_lo(tp * 2 + (i + 1))
                        finish(tp, i)
                if b + 1 < B:
                    normalise(b + 1, 0)
                hidden_lo(NT - 1)
                if b + 1 < B:
                    normalise(b + 1, 1)
                finish(NT // 2 - 1, 0)
                finish(NT // 2 - 1, 1)

            dve.wait_ge(const_ready, 4)
            for b in range(B):
                project(b)
                end_phase(dve, 3 * b + 1)
                heads(b)
                end_phase(dve, 3 * b + 2)
                tail(b)
                end_phase(dve, 3 * b + 3)

        @block.tensor
        def _(pe):
            begin_at_one(pe, scores_ps, pv_done, ffn_ps, *h_used)
            def three(o, a_hi, a_lo, b_hi, b_lo, first, last):
                pe.matmul(o, a_hi, b_hi, start=first, stop=False)
                pe.matmul(o, a_hi, b_lo, start=False, stop=False)
                return pe.matmul(o, a_lo, b_hi, start=False, stop=last)

            def project(b):
                def transpose(t):
                    pe.wait_ge(xn_done, b * NT + t + 1)
                    if t >= 2:
                        pe.wait_ge(xt_lo_done, b * NT + t - 1)
                    for kt in range(KT):
                        mm = pe.transpose(SB[t % 2][:, 0, kt * P:(kt + 1) * P], xb[:, t, kt * P:(kt + 1) * P],
                                          ident[:])
                    mm.then_inc(xt_ps, 1)

                def group(g):
                    if g >= 4:
                        pe.wait_ge(proj_lo_done, b * NG + g - 3)
                    o = group_bank(g)
                    if g < NQK:
                        c, m, r = QK_GROUPS[g]
                        pe.wait_ge(xt_lo_done, b * NT + (c + 1) * TPC)
                        pe.wait_ge(split_lo, split_no(b, (m + 1) * KT))
                    else:
                        t, m = g - NQK, 2
                        pe.wait_ge(split_lo, split_no(b, NQ))
                    for kt in range(KT):
                        if g < NQK:
                            a = [w[m][:, kt, r * P:(r + 1) * P] for w in (w_hi, w_lo)]
                            v = [xt[:, kt, c * W:(c + 1) * W] for xt in (xt_hi, xt_lo)]
                        else:
                            a = [xt[:, kt, t * P:(t + 1) * P] for xt in (xt_hi, xt_lo)]
                            v = [w[m][:, kt, :] for w in (w_hi, w_lo)]
                        mm = three(o, *a, *v, kt == 0, kt == KT - 1)
                    mm.then_inc(proj_ps, 1)

                for t in range(TPC):
                    transpose(t)
                for t in range(TPC, NT):
                    group(t - TPC)
                    transpose(t)
                for g in range(TPC, NG):
                    group(g)
                    t = g - NQK
                    if t == MAX_TILE:
                        pe.wait_ge(stack_in[0], (b * NH // 2 + 1) * 32)
                    if t >= MAX_TILE:
                        for r in range(2 * (t - MAX_TILE), 2 * (t - MAX_TILE) + 2):
                            maxima(Head(0, b * NH), r)
                transpose_maxima(Head(0, b * NH))

            def maxima(h, r):
                t, q, k = MAX_ORDER[r], q_st[h.buf], k_st[h.buf]
                end = (t + 1) * P
                if r >= 2:
                    pe.wait_ge(max_done, h.count(NT, r - 1))
                for at in range(0, end, W):
                    width = min(W, max(end - at, 2 * P))
                    mm = pe.matmul(max_bank(t)[:, at:at + width], q[0:STACK, t * P:(t + 1) * P],
                                   k[0:STACK, at:at + width], start=True, stop=True)
                mm.then_inc(max_ps, 1)

            def transpose_maxima(h):
                pe.wait_ge(max_done, h.count(NT, NT))
                pe.transpose(X[0:NT, 0, 0:P], mx[:], ident[:]).then_inc(mt_ps, 1)

            def scores(h, s):
                c, k = STEPS[s]
                start, _, end = score_cols(c, k)
                if s != 1:
                    pe.wait_ge(exp_done, h.count(NS, max(s - 1, 0)))
                pe.matmul(SB[s % 2][:, 0, 0:end - start], k_st[h.buf][0:STACK + 2, k * P:(k + 1) * P],
                          q_st[h.buf][0:STACK + 2, start:end], start=True, stop=True).then_inc(scores_ps, 1)

            def context(h, s):
                c, k = STEPS[s]
                _, need, end = score_cols(c, k)
                if k == 0:
                    pe.wait_ge(o_read, h.count(NC, c))
                wait_lo(pe, h, s)
                for t in range(need // P, end // P):
                    at = t * P - need
                    o = (t - c * TPC) * VC
                    pe.matmul(O[:, 0, o:o + VC], p_hi[s % NP][:, at:at + P], vh[h.buf][:, k, :],
                              start=k == 0 and t == c * TPC, stop=False, skip_group_check=True)
                    mm = pe.matmul(O[:, 0, o + DH:o + VC], p_lo[s % NP][:, at:at + P], vh[h.buf][:, k, DH:VC],
                                   start=False, stop=t == k, skip_group_check=True)
                mm.then_inc(pv_done, 1)

            def ffn(h, first, end):
                for i in range(first, end):
                    g, k = divmod(i, GMM)
                    c, m = divmod(g, 2)
                    kt, p = divmod(k, 3)
                    if i == 0:
                        pe.wait_ge(w13_lo_done, h.count(1, 1))
                    if k == 0:
                        pe.wait_ge(hidden_done if m else gate_done, h.count(NC, c))
                    w = (w13_hi, w13_hi, w13_lo)[p][h.buf][:, m, kt * P:(kt + 1) * P]
                    v = (xt_hi, xt_lo, xt_hi)[p][:, kt, c * W:(c + 1) * W]
                    mm = pe.matmul(F[m][:, 0, :], w, v, start=k == 0, stop=k == GMM - 1)
                    if k == GMM - 1:
                        mm.then_inc(ffn_ps, 1)

            def head_step(jj, u, n0, last=False):
                h = Head(jj, n0 + u)
                ffn(h, 0, FFN_UPTO[0])
                pe.wait_ge(m_in, h.count(32, 32))
                pe.wait_ge(vh_ready, h.count0(1, 1))
                for s in range(NS + LAG):
                    if s < NS:
                        scores(h, s)
                    if s > 0:
                        ffn(h, FFN_UPTO[s - 1], FFN_UPTO[s])
                    if not last and MAX_SLOT <= s < MAX_SLOT + NT:
                        if s == MAX_SLOT:
                            pe.wait_ge(stack_in[1 - u], jj * 32 + (n0 // 2 + 1 + u) * 32)
                        maxima(h.next(), s - MAX_SLOT)
                    if s >= LAG:
                        context(h, s - LAG)
                    if not last and s == MT_SLOT:
                        transpose_maxima(h.next())

            def heads(b):
                n0 = b * NH
                pe.wait_ge(ones_ready, 3 * (b + 1))
                with pe.Fori(0, NH // 2 - 1) as jj:
                    head_step(jj, 0, n0)
                    head_step(jj, 1, n0)
                head_step(NH // 2 - 1, 0, n0)
                head_step(NH // 2 - 1, 1, n0, last=True)

            def tail(b):
                def transpose(t):
                    if t >= 2:
                        pe.wait_ge(ct_lo_done, b * NT + t - 1)
                    for kt in range(KT):
                        mm = pe.transpose(SB[t % 2][:, 0, kt * P:(kt + 1) * P],
                                          ctx_nat[:, t, kt * P:(kt + 1) * P], ident[:])
                    mm.then_inc(ct_ps, 1)

                def hadamard_128(a):
                    k = stage_no(0, NQ + NO) + a
                    pe.wait_ge(stage_in[k % 3], stage_count(k))
                    if a >= 2:
                        pe.wait_ge(g_lo_done, a - 1)
                    pe.matmul(F[a % 2][:, 0, :], had[:], stage[k % 3][:], start=True, stop=True
                              ).then_inc(had_ps, 1)

                def attention_out(t):
                    if t == 0:
                        pe.wait_ge(split_lo, split_no(b, NQ + NO))
                    pe.wait_ge(ct_lo_done, b * NT + t + 1)
                    if t >= 2:
                        pe.wait_ge(attn_done, b * NT + t - 1)
                    for kt in range(KT):
                        mm = three(M[:, t % 2, :], ct_hi[t % 2][:, kt, :], ct_lo[t % 2][:, kt, :],
                                   wo_hi[:, kt, :], wo_lo[:, kt, :], kt == 0, kt == KT - 1)
                    mm.then_inc(attn_ps, 1)

                transpose(0)
                for t in range(NT):
                    if t + 1 < NT:
                        transpose(t + 1)
                    if b == 0:
                        hadamard_128(2 * t)
                        hadamard_128(2 * t + 1)
                    attention_out(t)

                def down(tp, i):
                    t = tp * 2 + i
                    pe.wait_ge(silu_a[i], 1 + tp + b * NT // 2)
                    for h in range(2):
                        pe.wait_ge(h_lo_done[h], t + (b * NT + 1))
                        for k in range(JT // 2):
                            j = h * (JT // 2) + k
                            mm = three(F[i][:, 0, :], h_hi[h][:, k, :], h_lo[h][:, k, :], g_hi[:, j, :],
                                       g_lo[:, j, :], j == 0, j == JT - 1)
                        mm.then_inc(h_used[h], 1)

                if b == 0:
                    pe.wait_ge(g_lo_done, JT)
                else:
                    pe.wait_ge(g_in, 32)
                with pe.Fori(0, NT // 2) as tp:
                    for i in range(2):
                        down(tp, i)

            pe.wait_ge(const_ready, 4)
            pe.wait_ge(had_in, 16)
            for b in range(B):
                project(b)
                end_phase(pe, 3 * b + 1)
                heads(b)
                end_phase(pe, 3 * b + 2)
                tail(b)
                end_phase(pe, 3 * b + 3)


def kernel(L0_attn_x, L0_attn_Wq, L0_attn_Wk, L0_attn_Wv, L0_attn_Wo, L0_ffn_W1, L0_ffn_W2, L0_ffn_W3):
    import numpy as np
    import concourse.bacc as bacc
    from concourse.bass_utils import run_bass_kernel_spmd

    def tiles(w):
        w = np.asarray(w).reshape(JT, P, KT, P)
        return np.ascontiguousarray(w.transpose(0, 3, 2, 1)).reshape(JT, P, D)

    sylvester = np.ones((1, 1), np.float32)
    while sylvester.shape[0] < P:
        sylvester = np.block([[sylvester, sylvester], [sylvester, -sylvester]])
    arrays = {
        "x": np.ascontiguousarray(L0_attn_x),
        "wq": np.ascontiguousarray(np.asarray(L0_attn_Wq).T),
        "wk": np.ascontiguousarray(np.asarray(L0_attn_Wk).T),
        "wv": np.ascontiguousarray(np.asarray(L0_attn_Wv).T),
        "wo": np.ascontiguousarray(np.asarray(L0_attn_Wo).T),
        "w1w3": np.ascontiguousarray(np.stack([tiles(L0_ffn_W1), tiles(L0_ffn_W3)], axis=2)),
        "w2": np.ascontiguousarray(np.asarray(L0_ffn_W2).T).reshape(JT, P, D),
        "hadamard": np.ascontiguousarray(sylvester),
    }
    nc = bacc.Bacc("TRN2", target_bir_lowering=False, num_devices=1)
    args = [nc.dram_tensor(n, a.shape, mybir.dt.from_np(a.dtype), kind="ExternalInput").ap()
            for n, a in arrays.items()]
    out = nc.dram_tensor("out", (B, S, D), F32, kind="ExternalOutput").ap()
    build(nc, *args, out)
    r = run_bass_kernel_spmd(nc, [arrays], core_ids=[0])
    return r.results[0]["out"]
```

```python
import concourse.bass as bass
from concourse import mybir
from contextlib import ExitStack

F32 = mybir.dt.float32
F32R = mybir.dt.float32r
F16 = mybir.dt.float16
BF16 = mybir.dt.bfloat16
ALU = mybir.AluOpType
ACT = mybir.ActivationFunctionType
AX = mybir.AxisListType

P = 128
B, S, D = 2, 1024, 512
HID = 2048
NH, DH = 16, 32
KT = D // P
JT = HID // P
NT = S // P
W = 512
NC = S // W
TPC = W // P
SCALE = float(DH) ** -0.5
EPS = 1e-5
W2_SCALE = 0.5 * float(HID) ** -0.5
MASKED = -1e38
VC = 98
VS = 3 * DH
STACK = 3 * DH
STEPS = [(c, k) for c in range(NC) for k in range(TPC * (c + 1))]
NS = len(STEPS)
MAX_ORDER = [7, 0, 6, 1, 5, 2, 4, 3]
LAG = 3
NP = LAG + 1
POOL_LO = [5, 7]
DVE_LO = [s for s in range(NS) if s not in POOL_LO]
MAX_SLOT = 3
MT_SLOT = 11
MAX_BEFORE = {3: [0], 4: [1, 2], 5: [3, 4], 6: [5, 6], 7: [7]}
NB = 4
GROUPS = 4
GMM = 3 * KT
FFN_UPTO = [9, 12, 15, 17, 19, 21, 23, 26, 28, 30, 33, 38, 42, 45, 48]
HIDE_SLOT = 8
GATE_AT = {4: 0, 12: 1}
TANH_AT = {3: 0, 12: 1}


def build(nc, x, wq, wk, wv, wo, w1w3, w2, hadamard, out):
    stacks = nc.dram_tensor("qk_stacks", [2, 3, D, S], F32R, kind="Internal").ap()
    w2b_dram = nc.dram_tensor("w2_butterflied", [JT, P, D], F32, kind="Internal").ap()
    g_dram = nc.dram_tensor("w2_transformed", [2, P, JT, D], F32R, kind="Internal").ap()

    ctx = ExitStack()
    with ctx:
        def sb(name, shape, dt, stack=ctx):
            return stack.enter_context(nc.sbuf_tensor(name, shape, dt))

        def bank(name, banks=1):
            return ctx.enter_context(nc.psum_tensor(name, [P, banks, W], F32))

        def sem(name):
            return ctx.enter_context(nc.semaphore(name))

        ident = sb("ident", [P, P], F32)
        had = sb("had", [P, P], F32)
        causal = sb("causal", [P, S], BF16)
        ctx_nat = sb("ctx_nat", [P, NT, D], F32)
        w13 = sb("w13", [P, 2, D], F32)
        stage = [sb(f"stage{i}", [P, D], F32) for i in range(3)]
        stats = sb("stats", [P, NT, 6], F32)
        mv = sb("mv", [P, NT, 2], F32)
        var, std, rstd, tmp = (sb(n, [P, NT], F32) for n in ("var", "std", "rstd", "tmp"))

        with ExitStack() as r:
            hidden = sb("hidden", [P, JT, S], F32, r)
        w_hi = [sb(f"w{m}_hi", [P, KT, D], F32R) for m in range(3)]
        w_lo = [sb(f"w{m}_lo", [P, KT, D], F32R) for m in range(3)]
        wht_in = [sb(f"wht_in{i}", [P, JT, P], F32) for i in range(2)]

        with ExitStack() as r:
            xb = sb("xb", [P, NT, D], F32, r)
        with ExitStack() as r:
            q_st = [sb(f"q_st{i}", [P, S], F32R, r) for i in range(2)]
            k_st = [sb(f"k_st{i}", [P, S], F32R, r) for i in range(2)]
        wo_hi = sb("wo_hi", [P, KT, D], F32R)
        wo_lo = sb("wo_lo", [P, KT, D], F32R)

        with ExitStack() as r:
            xt_hi = sb("xt_hi", [P, KT, S], F32R, r)
            xt_lo = sb("xt_lo", [P, KT, S], F32R, r)
            vparts = sb("vparts", [P, NT, NH, VC], BF16, r)
            mx = sb("mx", [P, NT], F32, r)
            m_hi = sb("m_hi", [NT, P], F32R, r)
            m_lo = sb("m_lo", [NT, P], F32R, r)
            w13_hi0 = sb("w13_hi0", [P, 2, D], F32R, r)
            w13_lo0 = sb("w13_lo0", [P, 2, D], F32R, r)
            with ExitStack() as q:
                qk_hi = [sb(f"qk_hi{i}", [P, W], F32R, q) for i in range(NB)]
                qk_lo = [sb(f"qk_lo{i}", [P, W], F32R, q) for i in range(NB)]
                vrest = [sb(f"vrest{i}", [P, W], F32, q) for i in range(2)]
                wht_mid = sb("wht_mid", [P, JT, P], F32, q)
            w13_hi = [w13_hi0, sb("w13_hi1", [P, 2, D], F32R, r)]
            w13_lo = [w13_lo0, sb("w13_lo1", [P, 2, D], F32R, r)]
            expd = [sb(f"expd{i}", [P, W], F32, r) for i in range(NP)]
            p_hi = [sb(f"p_hi{i}", [P, W], F16, r) for i in range(NP)]
            p_lo = [sb(f"p_lo{i}", [P, W], F16, r) for i in range(NP)]
            gate_t = sb("gate_t", [P, W], F32, r)
            gate_a = sb("gate_a", [P, W], F32, r)
            vh = [sb(f"vh{i}", [P, NT, VC], BF16, r) for i in range(2)]
            ctx_raw = [sb(f"ctx_raw{i}", [P, TPC, DH], F32, r) for i in range(NC)]
            rden = [sb(f"rden{i}", [P, TPC], F32, r) for i in range(NC)]
        g_hi = sb("g_hi", [P, JT, D], F32R)
        g_lo = sb("g_lo", [P, JT, D], F32R)
        h_hi = [sb(f"h_hi{i}", [P, JT // 2, P], F32R) for i in range(2)]
        h_lo = [sb(f"h_lo{i}", [P, JT // 2, P], F32R) for i in range(2)]
        had_r = sb("had_r", [P, P], F32R)
        ct_hi = [sb(f"ct_hi{i}", [P, KT, P], F32R) for i in range(2)]
        ct_lo = [sb(f"ct_lo{i}", [P, KT, P], F32R) for i in range(2)]
        x_in = [sb(f"x_in{i}", [P, D], F32) for i in range(2)]
        y = [sb(f"y{i}", [P, D], F32) for i in range(2)]

        F = [bank("f0"), bank("f1")]
        SB = [bank("s0"), bank("s1")]
        M = bank("m", 2)
        X = bank("xs")
        O = bank("o")

        const_ready = sem("const_ready")
        had_in = sem("had_in")
        phase_done = sem("phase_done")
        x_loaded = [sem(f"x_loaded{i}") for i in range(NT // 2)]
        stage_in = [sem(f"stage_in{i}") for i in range(3)]
        split_hi, split_lo = sem("split_hi"), sem("split_lo")
        stats_done, mv_done, var_done, sqrt_done, newton = (
            sem(n) for n in ("stats_done", "mv_done", "var_done", "sqrt_done", "newton"))
        xn_done, xt_ps, xt_hi_done, xt_lo_done = (
            sem(n) for n in ("xn_done", "xt_ps", "xt_hi_done", "xt_lo_done"))
        proj_ps, proj_hi_done, proj_lo_done = (sem(n) for n in ("proj_ps", "proj_hi_done", "proj_lo_done"))
        v2_done, v3_done = sem("v2_done"), sem("v3_done")
        wo_in = sem("wo_in")
        qk_stored = [sem(f"qk_stored{i}") for i in range(NB)]
        wht_loaded, wht_step, wht_stored = sem("wht_loaded"), sem("wht_step"), sem("wht_stored")
        ones_ready = sem("ones_ready")
        stack_in = [sem(f"stack_in{i}") for i in range(2)]
        max_ps, max_done, mt_ps, m_hi_done, m_lo_done, m_in = (
            sem(n) for n in ("max_ps", "max_done", "mt_ps", "m_hi_done", "m_lo_done", "m_in"))
        scores_ps, exp_done, mask_done, p_hi_done, p_lo_done, p_lo_pool, pv_done = (
            sem(n) for n in ("scores_ps", "exp_done", "mask_done", "p_hi_done", "p_lo_done", "p_lo_pool", "pv_done"))
        max_begun, mask_begun = sem("max_begun"), sem("mask_begun")
        o_read, ctx_done, vh_ready = sem("o_read"), sem("ctx_done"), sem("vh_ready")
        w13_in, w13_hi_done, w13_lo_done = sem("w13_in"), sem("w13_hi_done"), sem("w13_lo_done")
        ffn_ps, tanh_done, gate_done, hidden_done = (
            sem(n) for n in ("ffn_ps", "tanh_done", "gate_done", "hidden_done"))
        ct_ps, ct_hi_done, ct_lo_done, attn_ps, attn_done = (
            sem(n) for n in ("ct_ps", "ct_hi_done", "ct_lo_done", "attn_ps", "attn_done"))
        w2_hi, w2_lo = ([v[1][:].rearrange("p k c -> p (k c)")[:, i * D:(i + 1) * D] for i in range(2)]
                        for v in (h_hi, h_lo))
        had_ready, w2_hi_done, w2_lo_done = sem("had_ready"), sem("w2_hi_done"), sem("w2_lo_done")
        had_ps, g_hi_done, g_lo_done, g_stored, g_in = (
            sem(n) for n in ("had_ps", "g_hi_done", "g_lo_done", "g_stored", "g_in"))
        h_hi_done = [sem(f"h_hi_done{i}") for i in range(2)]
        h_lo_done = [sem(f"h_lo_done{i}") for i in range(2)]
        h_used = [sem(f"h_used{i}") for i in range(2)]
        silu_t, silu_s = sem("silu_t"), sem("silu_s")
        silu_a = [sem(f"silu_a{i}") for i in range(2)]
        x_again = [sem(f"x_again{i}") for i in range(2)]
        y_done = [sem(f"y_done{i}") for i in range(2)]
        y_stored = [sem(f"y_stored{i}") for i in range(2)]

        block = ctx.enter_context(nc.Block())

        NQ, NO = 3 * KT, KT - 2

        def stage_no(b, i):
            return b * (NQ + NO + JT) + i

        def split_no(b, i):
            return b * (NQ + NO + 1) + i

        def stage_count(k):
            return (k // 3 + 1) * 16

        def begin_at_one(e, *counters):
            for s in counters:
                e.sem_inc(s, 1)

        ENGINES = 5

        def end_phase(e, n):
            e.drain().then_inc(phase_done, 1)
            e.wait_ge(phase_done, ENGINES * n)

        QK_GROUPS = ([(c, m, o) for c in range(NC - 1) for m in range(2) for o in range(KT)]
                     + [(NC - 1, m, o) for o in range(KT) for m in range(2)])
        NQK = len(QK_GROUPS)
        NG = NQK + NT
        FIRST_HEAD_GROUP = NQK - 2 * KT + 1
        FIRST_STACK = FIRST_HEAD_GROUP + 2

        def group_bank(g):
            return (F[0], F[1], O, X if g < NQK else SB[0])[g % 4][:, 0, :]

        def score_cols(c, k):
            need, end = max(c * W, k * P), (c + 1) * W
            return min(need, end - 2 * P), need, end

        def max_bank(t):
            return M[:].rearrange("p b w -> p (b w)") if t >= TPC else X[:, 0, :]

        class Head:

            def __init__(self, jj, m):
                self.jj, self.m, self.buf = jj, m, m % 2

            def next(self):
                return Head(self.jj, self.m + 1)

            def count(self, each, more=0):
                return self.jj * (2 * each) + (self.m * each + more + 1)

            def count0(self, each, more):
                return self.jj * (2 * each) + (self.m * each + more)

        def wait_lo(e, h, s):
            if s in POOL_LO:
                e.wait_ge(p_lo_pool, h.count(len(POOL_LO), POOL_LO.index(s) + 1))
            else:
                e.wait_ge(p_lo_done, h.count(len(DVE_LO), DVE_LO.index(s) + 1))

        def load_stack(sp, head, buf):
            for which, dst in enumerate((q_st, k_st)):
                sp.dma_start(dst[buf][0:STACK, :].bitcast(F32),
                             stacks[which, :, bass.ds(head * DH, DH), :].bitcast(F32)
                             ).then_inc(stack_in[buf], 16)

        @block.sync
        def _(sp):
            begin_at_one(sp, m_in, *y_stored)

            def load_weight(b, i):
                if i >= 3:
                    sp.wait_ge(split_lo, split_no(b, i) - 2)
                k = stage_no(b, i)
                sp.dma_start(stage[k % 3][:], (wq, wk, wv, wo)[i // KT][i % KT * P:(i % KT + 1) * P, :]
                             ).then_inc(stage_in[k % 3], 16)

            def load_first(b):
                xv = x[b].rearrange("(t p) d -> p t d", p=P)

                def load_pair(i):
                    sp.dma_start(xb[:, 2 * i:2 * i + 2, :], xv[:, 2 * i:2 * i + 2, :]
                                 ).then_inc(x_loaded[i], 16)

                load_pair(0)
                load_pair(1)
                for i in range(3):
                    load_weight(b, i)
                load_pair(2)
                load_pair(3)

            def load_slab(s):
                if s >= 2:
                    sp.wait_ge(wht_stored, (s - 1) * 16)
                sp.dma_start(wht_in[s % 2][:], w2[:, :, s * P:(s + 1) * P].rearrange("a p d -> p a d")
                             ).then_inc(wht_loaded, 16)

            def store_slab(s):
                sp.wait_ge(wht_step, (s + 1) * 8)
                sp.dma_start(w2b_dram[:, :, s * P:(s + 1) * P].rearrange("a p d -> p a d"), wht_in[s % 2][:]
                             ).then_inc(wht_stored, 16)

            SLABS = {3: (store_slab, 0), 5: (load_slab, 2), 6: (store_slab, 1), 8: (load_slab, 3)}

            def project(b):
                for i in range(3, 2 * KT + 3):
                    load_weight(b, i)
                    if b == 0 and i == 2 * KT:
                        load_slab(1)
                for g, (c, m, o) in enumerate(QK_GROUPS):
                    if g >= KT and 2 * KT + 3 + g - KT < NQ:
                        load_weight(b, 2 * KT + 3 + g - KT)
                    sp.wait_ge(proj_lo_done, b * NG + g + 1)
                    for part, src in enumerate((qk_hi, qk_lo, qk_hi) if m else (qk_hi, qk_hi, qk_lo)):
                        sp.dma_start(stacks[m, part, o * P:(o + 1) * P, c * W:(c + 1) * W].bitcast(F32),
                                     src[g % NB][:].bitcast(F32)).then_inc(qk_stored[g % NB], 16)
                    if b == 0 and g in SLABS:
                        step, slab = SLABS[g]
                        step(slab)
                    if g == KT:
                        load_w13(0, Head(0, b * NH))
                    if g == FIRST_STACK:
                        for i in range(NB):
                            sp.wait_ge(qk_stored[i], (b * (NQK // NB) + (FIRST_HEAD_GROUP - i) // NB + 1) * 48)
                        load_stack(sp, 0, 0)
                for i in range(NQ, NQ + NO):
                    load_weight(b, i)
                for i in range(NB):
                    sp.wait_ge(qk_stored[i], (b + 1) * (NQK // NB) * 48)
                if b == 0:
                    store_slab(2)
                load_w13(1, Head(0, b * NH + 1))
                if b > 0:
                    for i in range(2):
                        sp.wait_ge(y_stored[i], 1 + b * (NT // 2) * 16)
                store_maxima(Head(0, b * NH))
                if b == 0:
                    store_slab(3)

            def load_w13(j, h):
                sp.wait_ge(w13_lo_done, h.count(1))
                sp.dma_start(w13[:], w1w3[bass.ds(j, 1)]).then_inc(w13_in, 16)

            def store_maxima(h):
                sp.wait_ge(m_lo_done, h.count0(1, 1))
                for row, part in ((STACK, m_hi), (STACK + 1, m_lo)):
                    sp.dma_start(q_st[h.buf][row:row + 1, :].rearrange("o (t p) -> o t p", p=P).bitcast(F32),
                                 part[:].bitcast(F32)).then_inc(m_in, 16)

            def head_step(jj, u, n0, last=False):
                j, h = jj * 2 + u, Head(jj, n0 + u)
                sp.wait_ge(scores_ps, h.count(NS))
                load_stack(sp, j + 1, 1 - u)
                if not last:
                    load_w13(j + 2, h.next().next())
                store_maxima(h.next())

            def heads(b):
                n0 = b * NH
                if b == 0:
                    sp.wait_ge(wht_stored, D // P * 16)
                with sp.Fori(0, NH // 2 - 1) as jj:
                    head_step(jj, 0, n0)
                    head_step(jj, 1, n0)
                head_step(NH // 2 - 1, 0, n0, last=True)
                sp.wait_ge(w13_lo_done, Head(0, n0 + NH).count(1))
                sp.dma_start(w13[:], wo[NO * P:KT * P, :].rearrange("(k p) d -> p k d", p=P)
                             ).then_inc(wo_in, 16)

            def tail(b):
                if b == 0:
                    for a in range(JT + 5):
                        if a < JT:
                            if a < 3:
                                sp.wait_ge(split_lo, split_no(0, NQ + NO) + a - 2)
                            else:
                                sp.wait_ge(w2_lo_done, a - 2)
                            k = stage_no(0, NQ + NO) + a
                            sp.dma_start(stage[k % 3][:], w2b_dram[a]).then_inc(stage_in[k % 3], 16)
                        if a >= 5:
                            sp.wait_ge(g_lo_done, a - 4)
                            for part, src in ((0, g_hi), (1, g_lo)):
                                sp.dma_start(g_dram[part, :, a - 5, :].bitcast(F32),
                                             src[:, a - 5, :].bitcast(F32)).then_inc(g_stored, 16)
                else:
                    sp.wait_ge(g_stored, 2 * JT * 16)
                    for part, dst in ((0, g_hi), (1, g_lo)):
                        sp.dma_start(dst[:].bitcast(F32), g_dram[part].bitcast(F32)).then_inc(g_in, 16)

                def load_x(t, i):
                    sp.dma_start(x_in[i][:], x[b, bass.ds(t * P, P), :]).then_inc(x_again[i], 16)

                def store_y(tp, i):
                    sp.wait_ge(y_done[i], tp + (b * NT // 2 + 1))
                    sp.dma_start(out[b, bass.ds((tp * 2 + i) * P, P), :], y[i][:]).then_inc(y_stored[i], 16)

                load_x(0, 0)
                load_x(1, 1)
                if b + 1 < B:
                    sp.wait_ge(attn_ps, (b + 1) * NT)
                    load_first(b + 1)
                with sp.Fori(0, NT // 2 - 1) as tp:
                    for i in range(2):
                        store_y(tp, i)
                        load_x(tp * 2 + (i + 2), i)
                for i in range(2):
                    store_y(NT // 2 - 1, i)
                if b + 1 == B:
                    for i in range(2):
                        sp.wait_ge(y_stored[i], 1 + (b + 1) * (NT // 2) * 16)

            load_first(0)
            load_slab(0)
            sp.dma_start(had[:], hadamard).then_inc(had_in, 16)
            for b in range(B):
                project(b)
                end_phase(sp, 3 * b + 1)
                heads(b)
                end_phase(sp, 3 * b + 2)
                tail(b)
                end_phase(sp, 3 * b + 3)

        @block.gpsimd
        def _(pool):
            begin_at_one(pool, w13_lo_done, p_lo_pool, ctx_done)
            pool.memset(ident[:], 0.0).then_inc(const_ready, 1)
            pool.memset(causal[:], 0.0).then_inc(const_ready, 1)
            pool.wait_ge(const_ready, 2)
            pool.affine_select(out=ident[:], in_=ident[:], compare_op=ALU.not_equal, fill=1.0, base=0,
                               pattern=[[-1, P]], channel_multiplier=1).then_inc(const_ready, 1)
            pool.affine_select(out=causal[:, S - P:S], in_=causal[:, S - P:S], compare_op=ALU.is_ge,
                               fill=MASKED, base=0, pattern=[[-1, P]], channel_multiplier=1
                               ).then_inc(const_ready, 1)

            def transform_w2():
                done = 0
                for s in range(D // P):
                    pool.wait_ge(wht_loaded, (s + 1) * 16)
                    src, dst = wht_in[s % 2], wht_mid
                    for st in range(4):
                        h = 1 << st
                        sv = src[:].rearrange("p (g two h) d -> p g two (h d)", two=2, h=h)
                        dv = dst[:].rearrange("p (g two h) d -> p g two (h d)", two=2, h=h)
                        for half, op in ((0, ALU.add), (1, ALU.subtract)):
                            pool.tensor_tensor(dv[:, :, half, :], sv[:, :, 0, :], sv[:, :, 1, :], op
                                               ).then_inc(wht_step, 1)
                        done += 2
                        pool.wait_ge(wht_step, done)
                        src, dst = dst, src

            def mask(h, s):
                pool.wait_ge(exp_done, h.count(NS, s + 1))
                pool.sem_inc(mask_begun, 1)
                e = expd[s % NP][:, 0:P]
                pool.affine_select(out=e, in_=e, compare_op=ALU.is_ge, fill=0.0, base=0, pattern=[[1, P]],
                                   channel_multiplier=-1).then_inc(mask_done, 1)

            def w13_low(h):
                pool.wait_ge(w13_hi_done, h.count0(1, 1))
                pool.tensor_tensor(w13_lo[h.buf][:], w13[:], w13_hi[h.buf][:].bitcast(F32), ALU.subtract
                                   ).then_inc(w13_lo_done, 1)

            def head_v(j, h):
                pool.tensor_copy(vh[h.buf][:].bitcast(F32), vparts[:, :, bass.ds(j, 1), :].bitcast(F32)
                                 ).then_inc(vh_ready, 1)

            def probs_lo(h, s):
                c, k = STEPS[s]
                _, need, end = score_cols(c, k)
                pool.wait_ge(p_hi_done, h.count0(NS, s + 1))
                pool.tensor_tensor(p_lo[s % NP][:, 0:end - need], expd[s % NP][:, 0:end - need],
                                   p_hi[s % NP][:, 0:end - need], ALU.subtract).then_inc(p_lo_pool, 1)

            def scale_ctx(j, h, c):
                pool.wait_ge(o_read, h.count(NC, c + 1))
                pool.tensor_tensor(ctx_nat[:, c * TPC:(c + 1) * TPC, bass.ds(j * DH, DH)], ctx_raw[c][:],
                                   rden[c][:].unsqueeze(2).broadcast_to([P, TPC, DH]), ALU.mult
                                   ).then_inc(ctx_done, 1)

            def head_step(jj, u, n0, last=False):
                j, h = jj * 2 + u, Head(jj, n0 + u)
                for s in range(TPC):
                    mask(h, s)
                if not last:
                    w13_low(h.next())
                    pool.wait_ge(pv_done, h.count(NS))
                    head_v(j + 1, h.next())
                for s in range(TPC, NS):
                    if s in POOL_LO:
                        probs_lo(h, s)
                    if s == TPC + LAG:
                        scale_ctx(j, h, 0)
                    if STEPS[s][1] >= TPC:
                        mask(h, s)
                scale_ctx(j, h, 1)

            def heads(b):
                n0 = b * NH
                head_v(0, Head(0, n0))
                with pool.Fori(0, NH // 2 - 1) as jj:
                    head_step(jj, 0, n0)
                    head_step(jj, 1, n0)
                head_step(NH // 2 - 1, 0, n0)
                head_step(NH // 2 - 1, 1, n0, last=True)

            for b in range(B):
                pool.memset(vparts[:, :, :, VS:VC], 1.0).then_inc(ones_ready, 1)
                if b == 0:
                    transform_w2()
                w13_low(Head(0, b * NH))
                end_phase(pool, 3 * b + 1)
                heads(b)
                end_phase(pool, 3 * b + 2)
                end_phase(pool, 3 * b + 3)

        @block.scalar
        def _(act):
            begin_at_one(act, exp_done)
            def split_weight(b, i):
                k = stage_no(b, i)
                act.wait_ge(stage_in[k % 3], stage_count(k))
                dst = wo_hi if i >= NQ else w_hi[i // KT]
                act.activation(dst[:, i % KT, :], stage[k % 3][:], ACT.Copy).then_inc(split_hi, 1)

            def root(b, half):
                c = slice(half * TPC, (half + 1) * TPC)
                act.wait_ge(var_done, 2 * b + half + 1)
                act.activation(std[:, c], var[:, c], ACT.Sqrt).then_inc(sqrt_done, 1)

            def project(b):
                def xt(t):
                    act.wait_ge(xt_ps, b * NT + t + 1)
                    act.activation(xt_hi[:, :, t * P:(t + 1) * P],
                                   SB[t % 2][:, 0, :].rearrange("p (k c) -> p k c", k=KT), ACT.Copy
                                   ).then_inc(xt_hi_done, 1)

                def qk(g):
                    act.wait_ge(proj_ps, b * NG + g + 1)
                    if b > 0 or g >= NB:
                        act.wait_ge(qk_stored[g % NB], (b * NQK + g) // NB * 48)
                    act.activation(qk_hi[g % NB][:], group_bank(g), ACT.Copy,
                                   scale=SCALE if QK_GROUPS[g][1] == 0 else 1.0).then_inc(proj_hi_done, 1)

                if b == 0:
                    root(b, 0)
                for t in range(TPC):
                    xt(t)
                    split_weight(b, t)
                root(b, 1)
                for i in range(KT, 2 * KT):
                    split_weight(b, i)
                for t in range(TPC, NT):
                    xt(t)
                    qk(t - TPC)
                for i in range(2 * KT, 3 * KT - 1):
                    split_weight(b, i)
                for g in range(TPC, NQK):
                    qk(g)
                    if g == TPC + 2:
                        split_weight(b, 3 * KT - 1)
                for t in range(NT + 1):
                    if t == 0:
                        w13_high(Head(0, b * NH))
                    if t < NT:
                        g = NQK + t
                        act.wait_ge(proj_ps, b * NG + g + 1)
                        act.activation(vparts[:, t, :, 2 * DH:3 * DH],
                                       group_bank(g).rearrange("p (h d) -> p h d", h=NH), ACT.Copy
                                       ).then_inc(proj_hi_done, 1)
                    if t >= 1:
                        act.wait_ge(proj_lo_done, b * NG + NQK + t)
                        act.activation(vparts[:, t - 1, :, DH:2 * DH],
                                       vrest[(t - 1) % 2][:].rearrange("p (h d) -> p h d", h=NH), ACT.Copy
                                       ).then_inc(v2_done, 1)
                maxima_hi(Head(0, b * NH))

            def exp(h, s):
                c, k = STEPS[s]
                start, need, end = score_cols(c, k)
                act.wait_ge(scores_ps, h.count(NS, s + 1))
                if s >= NP:
                    wait_lo(act, h, s - NP)
                elif s == 0:
                    act.wait_ge(p_lo_done, h.count(len(DVE_LO)))
                    act.wait_ge(p_lo_pool, h.count(len(POOL_LO)))
                act.activation(expd[s % NP][:, 0:end - need], SB[s % 2][:, 0, need - start:end - start],
                               ACT.Exp).then_inc(exp_done, 1)

            def probs_hi(h, s):
                c, k = STEPS[s]
                _, need, end = score_cols(c, k)
                act.wait_ge(exp_done, h.count(NS, s + 1))
                if k * P >= c * W:
                    act.wait_ge(mask_done, h.count0(NT, k + 1))
                act.wait_ge(pv_done, h.count(NS, max(s - NP + 1, 0)))
                act.activation(p_hi[s % NP][:, 0:end - need], expd[s % NP][:, 0:end - need], ACT.Copy
                               ).then_inc(p_hi_done, 1)

            def tanh(h, c):
                act.wait_ge(ffn_ps, h.count(GROUPS, 2 * c + 1))
                act.wait_ge(gate_done, h.count(NC, c))
                act.activation(gate_t[:], F[0][:, 0, :], ACT.Tanh, scale=0.5).then_inc(tanh_done, 1)

            def w13_high(h):
                act.wait_ge(w13_in, h.count0(16, 16))
                act.activation(w13_hi[h.buf][:], w13[:], ACT.Copy).then_inc(w13_hi_done, 1)

            def maxima_hi(h):
                act.wait_ge(mt_ps, h.count0(1, 1))
                act.wait_ge(m_in, h.count(32))
                act.activation(m_hi[:], X[0:NT, 0, 0:P], ACT.Copy, scale=-1.0).then_inc(m_hi_done, 1)

            def head_step(jj, u, n0, last=False):
                h = Head(jj, n0 + u)
                if not last:
                    act.wait_ge(ffn_ps, h.count(GROUPS))
                    w13_high(h.next())
                for s in range(NS + 1):
                    if s < NS:
                        exp(h, s)
                    if s >= 1:
                        probs_hi(h, s - 1)
                    if s in TANH_AT:
                        tanh(h, TANH_AT[s])
                    if not last and s == MT_SLOT + 1:
                        maxima_hi(h.next())

            def heads(b):
                n0 = b * NH
                act.preload_act_table(ACT.Exp)
                with act.Fori(0, NH // 2 - 1) as jj:
                    head_step(jj, 0, n0)
                    head_step(jj, 1, n0)
                head_step(NH // 2 - 1, 0, n0)
                head_step(NH // 2 - 1, 1, n0, last=True)

            def tail(b):
                def hidden_hi(t, halves=(0, 1)):
                    for i in halves:
                        act.wait_ge(h_used[i], 1 + t + b * NT)
                        act.activation(h_hi[i][:], hidden[:, i * (JT // 2):(i + 1) * (JT // 2), bass.ds(t * P, P)],
                                       ACT.Copy).then_inc(h_hi_done[i], 1)

                if b == 0:
                    act.wait_ge(had_in, 16)
                    act.activation(had_r[:], had[:], ACT.Copy).then_inc(had_ready, 1)
                for i in range(NQ, NQ + NO):
                    split_weight(b, i)
                act.wait_ge(wo_in, (b + 1) * 16)
                act.activation(wo_hi[:, NO:KT, :], w13[:], ACT.Copy).then_inc(split_hi, 1)

                def w2_high(a):
                    k = stage_no(0, NQ + NO) + a
                    act.wait_ge(stage_in[k % 3], stage_count(k))
                    if a >= 2:
                        act.wait_ge(had_ps, a - 1)
                    act.activation(w2_hi[a % 2], stage[k % 3][:], ACT.Copy).then_inc(w2_hi_done, 1)

                if b == 0:
                    w2_high(0)
                    w2_high(1)
                for t in range(NT + 1):
                    if t < NT:
                        act.wait_ge(ct_ps, b * NT + t + 1)
                        if t >= 2:
                            act.wait_ge(attn_ps, b * NT + t - 1)
                        act.activation(ct_hi[t % 2][:], SB[t % 2][:, 0, :].rearrange("p (k c) -> p k c", k=KT),
                                       ACT.Copy).then_inc(ct_hi_done, 1)
                        if t == NT - 1:
                            hidden_hi(0, (0,))
                        if b == 0:
                            for a in (2 * t, 2 * t + 1):
                                act.wait_ge(had_ps, a + 1)
                                act.activation(g_hi[:, a, :], F[a % 2][:, 0, :], ACT.Copy, scale=W2_SCALE
                                               ).then_inc(g_hi_done, 1)
                                if a + 2 < JT:
                                    w2_high(a + 2)
                    if t >= 1:
                        act.wait_ge(attn_ps, b * NT + t)
                        act.activation(ctx_nat[:, t - 1, :], M[:, (t - 1) % 2, :], ACT.Copy
                                       ).then_inc(attn_done, 1)

                def gate(tp, i):
                    act.wait_ge(h_used[1], 1 + tp * 2 + (i + 1 + b * NT))
                    act.wait_ge(y_stored[i], 1 + (tp + b * NT // 2) * 16)
                    act.activation(y[i][:], F[i][:, 0, :], ACT.Tanh, scale=0.5).then_inc(silu_t, 1)

                hidden_hi(0, (1,))
                with act.Fori(0, NT // 2 - 1) as tp:
                    for i in range(2):
                        hidden_hi(tp * 2 + (i + 1))
                        gate(tp, i)
                hidden_hi(NT - 1)
                if b + 1 < B:
                    root(b + 1, 0)
                gate(NT // 2 - 1, 0)
                gate(NT // 2 - 1, 1)

            for b in range(B):
                project(b)
                end_phase(act, 3 * b + 1)
                heads(b)
                end_phase(act, 3 * b + 2)
                tail(b)
                end_phase(act, 3 * b + 3)

        @block.vector
        def _(dve):
            begin_at_one(dve, p_lo_done, gate_done, hidden_done, o_read, max_done, *silu_a)
            def split_weight(b, i):
                k = stage_no(b, i)
                dve.wait_ge(split_hi, split_no(b, i) + 1)
                hi, lo = (wo_hi, wo_lo) if i >= NQ else (w_hi[i // KT], w_lo[i // KT])
                dve.tensor_tensor(lo[:, i % KT, :], stage[k % 3][:], hi[:, i % KT, :].bitcast(F32), ALU.subtract
                                  ).then_inc(split_lo, 1)

            def statistics(b, half):
                for t in range(half * TPC, (half + 1) * TPC):
                    if t % 2 == 0:
                        dve.wait_ge(x_loaded[t // 2], (b + 1) * 16)
                    dve.bn_stats(stats[:, t, :], xb[:, t, :]).then_inc(stats_done, 1)

            def normalise(b, half):
                tiles, c = range(half * TPC, (half + 1) * TPC), slice(half * TPC, (half + 1) * TPC)
                n = 2 * b + half
                for t in tiles:
                    dve.wait_ge(stats_done, b * NT + t + 1)
                    dve.bn_aggr(mv[:, t, :], stats[:, t, :]).then_inc(mv_done, 1)
                dve.wait_ge(mv_done, (n + 1) * TPC)
                dve.tensor_scalar(var[:, c], mv[:, c, 1], EPS, None, ALU.add).then_inc(var_done, 1)
                dve.wait_ge(sqrt_done, n + 1)
                dve.reciprocal(tmp[:, c], std[:, c]).then_inc(newton, 1)
                dve.wait_ge(newton, 5 * n + 1)
                dve.tensor_tensor(tmp[:, c], tmp[:, c], var[:, c], ALU.mult).then_inc(newton, 1)
                dve.wait_ge(newton, 5 * n + 2)
                dve.tensor_tensor(tmp[:, c], tmp[:, c], std[:, c], ALU.add).then_inc(newton, 1)
                dve.wait_ge(newton, 5 * n + 3)
                dve.tensor_scalar(tmp[:, c], tmp[:, c], 0.5, None, ALU.mult).then_inc(newton, 1)
                dve.wait_ge(newton, 5 * n + 4)
                dve.reciprocal(rstd[:, c], tmp[:, c]).then_inc(newton, 1)
                dve.wait_ge(newton, 5 * n + 5)
                for t in tiles:
                    dve.tensor_scalar(xb[:, t, :], xb[:, t, :], mv[:, t, 0:1], rstd[:, t:t + 1],
                                      ALU.subtract, ALU.mult).then_inc(xn_done, 1)

            def project(b):
                def xt(t):
                    dve.wait_ge(xt_hi_done, b * NT + t + 1)
                    at = (slice(None), slice(None), slice(t * P, (t + 1) * P))
                    dve.tensor_tensor(xt_lo[at], SB[t % 2][:, 0, :].rearrange("p (k c) -> p k c", k=KT),
                                      xt_hi[at].bitcast(F32), ALU.subtract).then_inc(xt_lo_done, 1)

                def qk(g):
                    dve.wait_ge(proj_hi_done, b * NG + g + 1)
                    ps, hi = group_bank(g), qk_hi[g % NB][:].bitcast(F32)
                    dve.scalar_tensor_tensor(qk_lo[g % NB][:], ps, SCALE if QK_GROUPS[g][1] == 0 else 1.0, hi,
                                             ALU.mult, ALU.subtract).then_inc(proj_lo_done, 1)

                if b == 0:
                    statistics(b, 0)
                    normalise(b, 0)
                for t in range(TPC):
                    xt(t)
                    split_weight(b, t)
                if b == 0:
                    statistics(b, 1)
                normalise(b, 1)
                for i in range(KT, 2 * KT):
                    split_weight(b, i)
                for t in range(TPC, NT):
                    xt(t)
                    qk(t - TPC)
                for i in range(2 * KT, 3 * KT - 1):
                    split_weight(b, i)
                for g in range(TPC, NQK):
                    qk(g)
                    if g == TPC + 2:
                        split_weight(b, 3 * KT - 1)
                    if g in (NQK - 6, NQK - 3):
                        dve.memset(k_st[g % 2][STACK:STACK + 2, :].bitcast(F32), 1.0).then_inc(ones_ready, 1)
                for t in range(NT + 1):
                    heads_of = lambda v: v.rearrange("p (h d) -> p h d", h=NH)
                    for r in MAX_BEFORE.get(t, []):
                        maxima(Head(0, b * NH), r)
                    if t < NT:
                        g = NQK + t
                        dve.wait_ge(proj_hi_done, b * NG + g + 1)
                        if t >= 2:
                            dve.wait_ge(v3_done, b * NT + t - 1)
                        dve.tensor_tensor(heads_of(vrest[t % 2][:]), heads_of(group_bank(g)),
                                          vparts[:, t, :, 2 * DH:3 * DH], ALU.subtract
                                          ).then_inc(proj_lo_done, 1)
                    if t >= 1:
                        dve.wait_ge(v2_done, b * NT + t)
                        dve.tensor_tensor(vparts[:, t - 1, :, 0:DH], heads_of(vrest[(t - 1) % 2][:]),
                                          vparts[:, t - 1, :, DH:2 * DH], ALU.subtract).then_inc(v3_done, 1)
                maxima_lo(Head(0, b * NH))

            def maxima(h, r):
                t = MAX_ORDER[r]
                width = (t + 1) * P
                dve.wait_ge(max_ps, h.count0(NT, r + 1))
                dve.sem_inc(max_begun, 1)
                dve.tensor_tensor_reduce(out=max_bank(t)[:, 0:width], in0=max_bank(t)[:, 0:width],
                                         in1=causal[:, S - width:S], scale=1.0, scalar=0.0, op0=ALU.add,
                                         op1=ALU.max, accum_out=mx[:, t:t + 1]).then_inc(max_done, 1)

            def maxima_lo(h):
                dve.wait_ge(m_hi_done, h.count0(1, 1))
                dve.scalar_tensor_tensor(m_lo[:], X[0:NT, 0, 0:P], -1.0, m_hi[:].bitcast(F32), ALU.mult,
                                         ALU.subtract).then_inc(m_lo_done, 1)

            def probs_lo(h, s):
                c, k = STEPS[s]
                _, need, end = score_cols(c, k)
                dve.wait_ge(p_hi_done, h.count0(NS, s + 1))
                dve.tensor_tensor(p_lo[s % NP][:, 0:end - need], expd[s % NP][:, 0:end - need],
                                  p_hi[s % NP][:, 0:end - need], ALU.subtract).then_inc(p_lo_done, 1)

            def read_ctx(h, c):
                dve.wait_ge(pv_done, h.count(NS, TPC if c == 0 else NS))
                dve.wait_ge(ctx_done, h.count(NC))
                o = O[:, 0, 0:TPC * VC].rearrange("p (t v) -> p t v", v=VC)
                dve.reciprocal(rden[c][:], o[:, :, VS])
                dve.tensor_reduce(ctx_raw[c][:], o[:, :, 0:VS].rearrange("p t (a d) -> p t d a", a=3),
                                  op=ALU.add, axis=AX.X).then_inc(o_read, 1)

            def gate(h, c):
                dve.wait_ge(tanh_done, h.count0(NC, c + 1))
                dve.wait_ge(hidden_done, h.count(NC, c))
                dve.scalar_tensor_tensor(gate_a[:], gate_t[:], 1.0, F[0][:, 0, :], ALU.add, ALU.mult
                                         ).then_inc(gate_done, 1)

            def hide(j, h, c):
                dve.wait_ge(gate_done, h.count(NC, c + 1))
                dve.wait_ge(ffn_ps, h.count(GROUPS, 2 * c + 2))
                dve.tensor_tensor(hidden[:, bass.ds(j, 1), c * W:(c + 1) * W], gate_a[:].unsqueeze(1),
                                  F[1][:], ALU.mult).then_inc(hidden_done, 1)

            def head_step(jj, u, n0, last=False):
                j, h = jj * 2 + u, Head(jj, n0 + u)
                for s in range(1, NS + 1):
                    if s == TPC + LAG - 1:
                        read_ctx(h, 0)
                    if not last and MAX_SLOT <= s < MAX_SLOT + NT:
                        maxima(h.next(), s - MAX_SLOT)
                    if s - 1 in DVE_LO:
                        probs_lo(h, s - 1)
                    if s in GATE_AT:
                        gate(h, GATE_AT[s])
                    if s == HIDE_SLOT:
                        hide(j, h, 0)
                    if not last and s == MT_SLOT + 1:
                        maxima_lo(h.next())
                read_ctx(h, 1)
                hide(j, h, 1)

            def heads(b):
                n0 = b * NH
                with dve.Fori(0, NH // 2 - 1) as jj:
                    head_step(jj, 0, n0)
                    head_step(jj, 1, n0)
                head_step(NH // 2 - 1, 0, n0)
                head_step(NH // 2 - 1, 1, n0, last=True)

            def tail(b):
                def hidden_lo(t, halves=(0, 1)):
                    for i in halves:
                        dve.wait_ge(h_hi_done[i], t + (b * NT + 1))
                        dve.tensor_tensor(h_lo[i][:],
                                          hidden[:, i * (JT // 2):(i + 1) * (JT // 2), bass.ds(t * P, P)],
                                          h_hi[i][:].bitcast(F32), ALU.subtract).then_inc(h_lo_done[i], 1)

                for i in range(NQ, NQ + NO):
                    split_weight(b, i)
                dve.wait_ge(split_hi, split_no(b, NQ + NO) + 1)
                dve.tensor_tensor(wo_lo[:, NO:KT, :], w13[:], wo_hi[:, NO:KT, :].bitcast(F32), ALU.subtract
                                  ).then_inc(split_lo, 1)

                def w2_low(a):
                    k = stage_no(0, NQ + NO) + a
                    dve.wait_ge(w2_hi_done, a + 1)
                    if a >= 2:
                        dve.wait_ge(had_ps, a - 1)
                    dve.tensor_tensor(w2_lo[a % 2], stage[k % 3][:], w2_hi[a % 2].bitcast(F32), ALU.subtract
                                      ).then_inc(w2_lo_done, 1)

                if b == 0:
                    w2_low(0)
                    w2_low(1)
                for t in range(NT):
                    dve.wait_ge(ct_hi_done, b * NT + t + 1)
                    dve.tensor_tensor(ct_lo[t % 2][:], SB[t % 2][:, 0, :].rearrange("p (k c) -> p k c", k=KT),
                                      ct_hi[t % 2][:].bitcast(F32), ALU.subtract).then_inc(ct_lo_done, 1)
                    if t == NT - 1:
                        hidden_lo(0, (0,))
                    if b == 0:
                        for a in (2 * t, 2 * t + 1):
                            dve.wait_ge(g_hi_done, a + 1)
                            dve.scalar_tensor_tensor(g_lo[:, a, :], F[a % 2][:, 0, :], W2_SCALE,
                                                     g_hi[:, a, :].bitcast(F32), ALU.mult, ALU.subtract
                                                     ).then_inc(g_lo_done, 1)
                            if a + 2 < JT:
                                w2_low(a + 2)

                def finish(tp, i):
                    t = tp * 2 + i
                    dve.wait_ge(silu_t, t + (b * NT + 1))
                    dve.scalar_tensor_tensor(y[i][:], y[i][:], 1.0, F[i][:, 0, :], ALU.add, ALU.mult
                                             ).then_inc(silu_a[i], 1)
                    dve.wait_ge(silu_a[i], 1 + tp + (b * NT // 2 + 1))
                    dve.tensor_tensor(y[i][:].unsqueeze(1), y[i][:].unsqueeze(1), ctx_nat[:, bass.ds(t, 1), :],
                                      ALU.mult).then_inc(silu_s, 1)
                    dve.wait_ge(silu_s, t + (b * NT + 1))
                    dve.wait_ge(x_again[i], (tp + (b * NT // 2 + 1)) * 16)
                    dve.scalar_tensor_tensor(y[i][:], y[i][:], 0.5, x_in[i][:], ALU.mult, ALU.add
                                             ).then_inc(y_done[i], 1)

                hidden_lo(0, (1,))
                dve.wait_ge(attn_done, (b + 1) * NT)
                with dve.Fori(0, NT // 2 - 1) as tp:
                    for i in range(2):
                        hidden_lo(tp * 2 + (i + 1))
                        finish(tp, i)
                if b + 1 < B:
                    statistics(b + 1, 0)
                hidden_lo(NT - 1)
                if b + 1 < B:
                    normalise(b + 1, 0)
                finish(NT // 2 - 1, 0)
                if b + 1 < B:
                    statistics(b + 1, 1)
                finish(NT // 2 - 1, 1)

            dve.wait_ge(const_ready, 4)
            for b in range(B):
                project(b)
                end_phase(dve, 3 * b + 1)
                heads(b)
                end_phase(dve, 3 * b + 2)
                tail(b)
                end_phase(dve, 3 * b + 3)

        @block.tensor
        def _(pe):
            begin_at_one(pe, scores_ps, pv_done, ffn_ps, *h_used)
            def three(o, a_hi, a_lo, b_hi, b_lo, first, last):
                pe.matmul(o, a_hi, b_hi, start=first, stop=False)
                pe.matmul(o, a_hi, b_lo, start=False, stop=False)
                return pe.matmul(o, a_lo, b_hi, start=False, stop=last)

            def transpose_xn(b, t):
                pe.wait_ge(xn_done, b * NT + t + 1)
                if t >= 2:
                    pe.wait_ge(xt_lo_done, b * NT + t - 1)
                for kt in range(KT):
                    mm = pe.transpose(SB[t % 2][:, 0, kt * P:(kt + 1) * P], xb[:, t, kt * P:(kt + 1) * P],
                                      ident[:])
                mm.then_inc(xt_ps, 1)

            def project(b):
                def group(g):
                    if g >= 4:
                        pe.wait_ge(proj_lo_done, b * NG + g - 3)
                    o = group_bank(g)
                    if g < NQK:
                        c, m, r = QK_GROUPS[g]
                        pe.wait_ge(xt_lo_done, b * NT + (c + 1) * TPC)
                        pe.wait_ge(split_lo, split_no(b, (m + 1) * KT))
                    else:
                        t, m = g - NQK, 2
                        pe.wait_ge(split_lo, split_no(b, NQ))
                    for kt in range(KT):
                        if g < NQK:
                            a = [w[m][:, kt, r * P:(r + 1) * P] for w in (w_hi, w_lo)]
                            v = [xt[:, kt, c * W:(c + 1) * W] for xt in (xt_hi, xt_lo)]
                        else:
                            a = [xt[:, kt, t * P:(t + 1) * P] for xt in (xt_hi, xt_lo)]
                            v = [w[m][:, kt, :] for w in (w_hi, w_lo)]
                        mm = three(o, *a, *v, kt == 0, kt == KT - 1)
                    mm.then_inc(proj_ps, 1)

                for t in range(0 if b == 0 else 2, TPC):
                    transpose_xn(b, t)
                for t in range(TPC, NT):
                    group(t - TPC)
                    transpose_xn(b, t)
                for g in range(TPC, NG):
                    if g - NQK in MAX_BEFORE:
                        pe.wait_ge(stack_in[0], (b * NH // 2 + 1) * 32)
                        pe.wait_ge(proj_lo_done, b * NG + NQK)
                        for r in MAX_BEFORE[g - NQK]:
                            maxima(Head(0, b * NH), r)
                    group(g)
                transpose_maxima(Head(0, b * NH))
                pe.wait_ge(proj_lo_done, (b + 1) * NG - NT // 2 + 1)
                ffn(Head(0, b * NH), 0, FFN_UPTO[0])

            def maxima(h, r):
                t, q, k = MAX_ORDER[r], q_st[h.buf], k_st[h.buf]
                end = (t + 1) * P
                if r >= 2:
                    pe.wait_ge(max_done, h.count(NT, r - 1))
                for at in range(0, end, W):
                    width = min(W, max(end - at, 2 * P))
                    mm = pe.matmul(max_bank(t)[:, at:at + width], q[0:STACK, t * P:(t + 1) * P],
                                   k[0:STACK, at:at + width], start=True, stop=True)
                mm.then_inc(max_ps, 1)

            def transpose_maxima(h):
                pe.wait_ge(max_done, h.count(NT, NT))
                pe.transpose(X[0:NT, 0, 0:P], mx[:], ident[:]).then_inc(mt_ps, 1)

            def scores(h, s):
                c, k = STEPS[s]
                start, _, end = score_cols(c, k)
                if s != 1:
                    pe.wait_ge(exp_done, h.count(NS, max(s - 1, 0)))
                pe.matmul(SB[s % 2][:, 0, 0:end - start], k_st[h.buf][0:STACK + 2, k * P:(k + 1) * P],
                          q_st[h.buf][0:STACK + 2, start:end], start=True, stop=True).then_inc(scores_ps, 1)

            def context(h, s):
                c, k = STEPS[s]
                _, need, end = score_cols(c, k)
                if k == 0:
                    pe.wait_ge(o_read, h.count(NC, c))
                wait_lo(pe, h, s)
                for t in range(need // P, end // P):
                    at = t * P - need
                    o = (t - c * TPC) * VC
                    pe.matmul(O[:, 0, o:o + VC], p_hi[s % NP][:, at:at + P], vh[h.buf][:, k, :],
                              start=k == 0 and t == c * TPC, stop=False, skip_group_check=True)
                    mm = pe.matmul(O[:, 0, o + DH:o + VC], p_lo[s % NP][:, at:at + P], vh[h.buf][:, k, DH:VC],
                                   start=False, stop=t == k, skip_group_check=True)
                mm.then_inc(pv_done, 1)

            def ffn(h, first, end):
                for i in range(first, end):
                    g, k = divmod(i, GMM)
                    c, m = divmod(g, 2)
                    kt, p = divmod(k, 3)
                    if i == 0:
                        pe.wait_ge(w13_lo_done, h.count(1, 1))
                    if k == 0:
                        pe.wait_ge(hidden_done if m else gate_done, h.count(NC, c))
                    w = (w13_hi, w13_hi, w13_lo)[p][h.buf][:, m, kt * P:(kt + 1) * P]
                    v = (xt_hi, xt_lo, xt_hi)[p][:, kt, c * W:(c + 1) * W]
                    mm = pe.matmul(F[m][:, 0, :], w, v, start=k == 0, stop=k == GMM - 1)
                    if k == GMM - 1:
                        mm.then_inc(ffn_ps, 1)

            def head_step(jj, u, n0, last=False):
                h = Head(jj, n0 + u)
                pe.wait_ge(m_in, h.count(32, 32))
                pe.wait_ge(vh_ready, h.count0(1, 1))
                for s in range(NS + LAG):
                    if s < NS:
                        scores(h, s)
                    if s > 0:
                        ffn(h, FFN_UPTO[s - 1], FFN_UPTO[s])
                    if not last and MAX_SLOT <= s < MAX_SLOT + NT:
                        if s == MAX_SLOT:
                            pe.wait_ge(stack_in[1 - u], jj * 32 + (n0 // 2 + 1 + u) * 32)
                        maxima(h.next(), s - MAX_SLOT)
                    if s >= LAG:
                        context(h, s - LAG)
                    if not last and s == MT_SLOT:
                        transpose_maxima(h.next())
                if not last:
                    ffn(h.next(), 0, FFN_UPTO[0])

            def heads(b):
                n0 = b * NH
                pe.wait_ge(ones_ready, 3 * (b + 1))
                with pe.Fori(0, NH // 2 - 1) as jj:
                    head_step(jj, 0, n0)
                    head_step(jj, 1, n0)
                head_step(NH // 2 - 1, 0, n0)
                head_step(NH // 2 - 1, 1, n0, last=True)

            def tail(b):
                def transpose(t):
                    if t >= 2:
                        pe.wait_ge(ct_lo_done, b * NT + t - 1)
                    for kt in range(KT):
                        mm = pe.transpose(SB[t % 2][:, 0, kt * P:(kt + 1) * P],
                                          ctx_nat[:, t, kt * P:(kt + 1) * P], ident[:])
                    mm.then_inc(ct_ps, 1)

                def hadamard_128(a):
                    if a == 0:
                        pe.wait_ge(had_ready, 1)
                    pe.wait_ge(w2_lo_done, a + 1)
                    if a >= 2:
                        pe.wait_ge(g_lo_done, a - 1)
                    pe.matmul(F[a % 2][:, 0, :], had_r[:], w2_hi[a % 2], start=True, stop=False)
                    pe.matmul(F[a % 2][:, 0, :], had_r[:], w2_lo[a % 2], start=False, stop=True
                              ).then_inc(had_ps, 1)

                def attention_out(t):
                    if t == 0:
                        pe.wait_ge(split_lo, split_no(b, NQ + NO) + 1)
                    pe.wait_ge(ct_lo_done, b * NT + t + 1)
                    if t >= 2:
                        pe.wait_ge(attn_done, b * NT + t - 1)
                    for kt in range(KT):
                        mm = three(M[:, t % 2, :], ct_hi[t % 2][:, kt, :], ct_lo[t % 2][:, kt, :],
                                   wo_hi[:, kt, :], wo_lo[:, kt, :], kt == 0, kt == KT - 1)
                    mm.then_inc(attn_ps, 1)

                transpose(0)
                for t in range(NT):
                    if t + 1 < NT:
                        transpose(t + 1)
                    if b == 0:
                        hadamard_128(2 * t)
                        hadamard_128(2 * t + 1)
                    attention_out(t)

                def down(tp, i):
                    t = tp * 2 + i
                    pe.wait_ge(silu_a[i], 1 + tp + b * NT // 2)
                    for h in range(2):
                        pe.wait_ge(h_lo_done[h], t + (b * NT + 1))
                        for k in range(JT // 2):
                            j = h * (JT // 2) + k
                            mm = three(F[i][:, 0, :], h_hi[h][:, k, :], h_lo[h][:, k, :], g_hi[:, j, :],
                                       g_lo[:, j, :], j == 0, j == JT - 1)
                        mm.then_inc(h_used[h], 1)

                if b == 0:
                    pe.wait_ge(g_lo_done, JT)
                else:
                    pe.wait_ge(g_in, 32)
                with pe.Fori(0, NT // 2) as tp:
                    for i in range(2):
                        down(tp, i)
                if b + 1 < B:
                    for t in range(2):
                        transpose_xn(b + 1, t)

            pe.wait_ge(const_ready, 4)
            for b in range(B):
                project(b)
                end_phase(pe, 3 * b + 1)
                heads(b)
                end_phase(pe, 3 * b + 2)
                tail(b)
                end_phase(pe, 3 * b + 3)


def kernel(L0_attn_x, L0_attn_Wq, L0_attn_Wk, L0_attn_Wv, L0_attn_Wo, L0_ffn_W1, L0_ffn_W2, L0_ffn_W3):
    import numpy as np
    import concourse.bacc as bacc
    from concourse.bass_utils import run_bass_kernel_spmd

    def tiles(w):
        w = np.asarray(w).reshape(JT, P, KT, P)
        return np.ascontiguousarray(w.transpose(0, 3, 2, 1)).reshape(JT, P, D)

    sylvester = np.ones((1, 1), np.float32)
    while sylvester.shape[0] < P:
        sylvester = np.block([[sylvester, sylvester], [sylvester, -sylvester]])
    arrays = {
        "x": np.ascontiguousarray(L0_attn_x),
        "wq": np.ascontiguousarray(np.asarray(L0_attn_Wq).T),
        "wk": np.ascontiguousarray(np.asarray(L0_attn_Wk).T),
        "wv": np.ascontiguousarray(np.asarray(L0_attn_Wv).T),
        "wo": np.ascontiguousarray(np.asarray(L0_attn_Wo).T),
        "w1w3": np.ascontiguousarray(np.stack([tiles(L0_ffn_W1), tiles(L0_ffn_W3)], axis=2)),
        "w2": np.ascontiguousarray(np.asarray(L0_ffn_W2).T).reshape(JT, P, D),
        "hadamard": np.ascontiguousarray(sylvester),
    }
    nc = bacc.Bacc("TRN2", target_bir_lowering=False, num_devices=1)
    args = [nc.dram_tensor(n, a.shape, mybir.dt.from_np(a.dtype), kind="ExternalInput").ap()
            for n, a in arrays.items()]
    out = nc.dram_tensor("out", (B, S, D), F32, kind="ExternalOutput").ap()
    build(nc, *args, out)
    r = run_bass_kernel_spmd(nc, [arrays], core_ids=[0])
    return r.results[0]["out"]
```
